# Optimizing a Trainium2 kernel written in Bass

```python
import numpy as np
import jax
import jax.numpy as jnp

def _softmax(x, axis=-1):
    return jax.nn.softmax(x, axis=axis)

def _gelu(x):
    return jax.nn.gelu(x, approximate=True)

def _silu(x):
    return jax.nn.silu(x)

def _sigmoid(x):
    return jax.nn.sigmoid(x)

def _layernorm(x, axis=-1, eps=1e-05):
    m = jnp.mean(x, axis=axis, keepdims=True)
    v = jnp.var(x, axis=axis, keepdims=True)
    return (x - m) / jnp.sqrt(v + eps)

def _scatter_add(tgt, idx, src, axis=0):
    return tgt.at[idx].add(src)

def _segment_sum(src, seg, n):
    return jax.ops.segment_sum(src, seg, n)
kernel_name = 'mk_decoder_postln_d1_seqx_r8_edb49f'

def setup_inputs(seed: int=0):
    np.random.seed(seed)
    _w = jnp.asarray

    def _rec_inputs():
        import jax
        import jax.numpy as jnp
        _rk = jax.random.key(seed)
        x = -0.0002928 + 1 * jax.random.normal(jax.random.fold_in(_rk, 1), (128, 64, 128), jnp.float32)
        _lenS = 64 - jax.random.randint(jax.random.fold_in(_rk, 7), (128,), 0, max(1, 64 // 4) + 1, jnp.int32)
        _lenS2 = 64 - jax.random.randint(jax.random.fold_in(_rk, 8), (128,), 0, max(1, 64 // 4) + 1, jnp.int32)
        _ctx_1024P = jax.random.normal(jax.random.fold_in(_rk, 11), (128, 16, 128), jnp.float32)
        _ctx_1024c = jax.random.dirichlet(jax.random.fold_in(_rk, 511), 0.3 * jnp.ones((16,), jnp.float32), (128, 64))
        _ctx_1024t = jnp.einsum('bsk,bkd->bsd', _ctx_1024c, _ctx_1024P)
        _ctx_1024t = _ctx_1024t * jax.lax.rsqrt(jnp.mean(jnp.square(_ctx_1024t)) + 1e-12) * 0.953939
        ctx_1024 = -1.39393e-06 + 0.999914 * (_ctx_1024t + 0.3 * jax.random.normal(jax.random.fold_in(_rk, 611), (128, 64, 128), jnp.float32))
        _validS = jnp.arange(64)[None, :] < _lenS[:, None]
        _validS2 = jnp.arange(64)[None, :] < _lenS2[:, None]
        _causal = jnp.tril(jnp.ones((64, 64), dtype=bool))
        mask_BxSxS2_bf0 = jnp.logical_not(jnp.ones((128, 64, 64), dtype=bool))
        return (x, ctx_1024, mask_BxSxS2_bf0)
    x, ctx_1024, mask_BxSxS2_bf0 = _rec_inputs()

    def _L0_attn_setup():
        import jax, jax.numpy as jnp
        import numpy as np
        HEAD = 8
        BLOCK = 64
        D_MODEL = 128
        key = jax.random.key(seed)
        ks = jax.random.split(key, 9)
        d = D_MODEL
        s = 0.02
        return {'src': jax.random.normal(ks[0], (4, 512, d), dtype=jnp.float32), 'Wq': jax.random.normal(ks[1], (d, d), dtype=jnp.float32) * s, 'bq': jax.random.normal(ks[2], (d,), dtype=jnp.float32) * s, 'Wk': jax.random.normal(ks[3], (d, d), dtype=jnp.float32) * s, 'bk': jax.random.normal(ks[4], (d,), dtype=jnp.float32) * s, 'Wv': jax.random.normal(ks[5], (d, d), dtype=jnp.float32) * s, 'bv': jax.random.normal(ks[6], (d,), dtype=jnp.float32) * s, 'Wo': jax.random.normal(ks[7], (d, d), dtype=jnp.float32) * s, 'bo': jax.random.normal(ks[8], (d,), dtype=jnp.float32) * s}
    _L0_attn_all = _L0_attn_setup()
    _L0_attn_in = {k: v for k, v in _L0_attn_all.items() if k in ('Wq', 'bq', 'Wk', 'bk', 'Wv', 'bv', 'Wo', 'bo')}
    del _L0_attn_all

    def _L0_xattn_setup():
        import jax, jax.numpy as jnp
        import numpy as np
        HIDDEN = 128
        HEADS = 16
        D_K = HIDDEN // HEADS
        SCALE = D_K ** (-0.5)
        B, S = (2, 256)
        key = jax.random.key(seed)
        ks = jax.random.split(key, 8)

        def xavier(k, shape):
            fan_out, fan_in = shape
            limit = (6.0 / (fan_in + fan_out)) ** 0.5
            return jax.random.uniform(k, shape, jnp.float32, -limit, limit)
        return {'q': jax.random.normal(ks[0], (B, S, HIDDEN), jnp.float32), 'k': jax.random.normal(ks[1], (B, S, HIDDEN), jnp.float32), 'v': jax.random.normal(ks[2], (B, S, HIDDEN), jnp.float32), 'mask': jnp.zeros((B, S, S), dtype=bool), 'Wq': xavier(ks[3], (HIDDEN, HIDDEN)), 'Wk': xavier(ks[4], (HIDDEN, HIDDEN)), 'Wv': xavier(ks[5], (HIDDEN, HIDDEN)), 'Wo': xavier(ks[6], (HIDDEN, HIDDEN))}
    _L0_xattn_all = _L0_xattn_setup()
    _L0_xattn_in = {k: v for k, v in _L0_xattn_all.items() if k in ('Wq', 'Wk', 'Wv', 'Wo')}
    del _L0_xattn_all

    def _L0_ffn_setup():
        import jax, jax.numpy as jnp
        import numpy as np
        B, T, D = (2, 256, 128)
        E, DFF, TOPK = (8, 512, 2)
        TEMPERATURE = 1.0
        key = jax.random.key(seed)
        k_x, k_w1, k_w2, k_r = jax.random.split(key, 4)
        x = jax.random.normal(k_x, (B, T, D), dtype=jnp.float32)
        W1 = jax.random.normal(k_w1, (E, DFF, D), dtype=jnp.float32) * 0.02
        W2 = jax.random.normal(k_w2, (E, D, DFF), dtype=jnp.float32) * 0.02
        Wr = jax.random.normal(k_r, (E, D), dtype=jnp.float32) * 0.02
        return {'x': x, 'W1': W1, 'W2': W2, 'Wr': Wr}
    _L0_ffn_all = _L0_ffn_setup()
    _L0_ffn_in = {k: v for k, v in _L0_ffn_all.items() if k in ('W1', 'W2', 'Wr')}
    del _L0_ffn_all
    return {'x': x, 'ctx_1024': ctx_1024, 'mask_BxSxS2_bf0': mask_BxSxS2_bf0, 'L0_attn_Wq': _L0_attn_in['Wq'], 'L0_attn_bq': _L0_attn_in['bq'], 'L0_attn_Wk': _L0_attn_in['Wk'], 'L0_attn_bk': _L0_attn_in['bk'], 'L0_attn_Wv': _L0_attn_in['Wv'], 'L0_attn_bv': _L0_attn_in['bv'], 'L0_attn_Wo': _L0_attn_in['Wo'], 'L0_attn_bo': _L0_attn_in['bo'], 'L0_xattn_Wq': _L0_xattn_in['Wq'], 'L0_xattn_Wk': _L0_xattn_in['Wk'], 'L0_xattn_Wv': _L0_xattn_in['Wv'], 'L0_xattn_Wo': _L0_xattn_in['Wo'], 'L0_ffn_W1': _L0_ffn_in['W1'], 'L0_ffn_W2': _L0_ffn_in['W2'], 'L0_ffn_Wr': _L0_ffn_in['Wr']}

def reference(x, ctx_1024, mask_BxSxS2_bf0, L0_attn_Wq, L0_attn_bq, L0_attn_Wk, L0_attn_bk, L0_attn_Wv, L0_attn_bv, L0_attn_Wo, L0_attn_bo, L0_xattn_Wq, L0_xattn_Wk, L0_xattn_Wv, L0_xattn_Wo, L0_ffn_W1, L0_ffn_W2, L0_ffn_Wr):
    import jax
    import jax.numpy as jnp

    def _L0_attn_ref(src, Wq, bq, Wk, bk, Wv, bv, Wo, bo):
        import jax, jax.numpy as jnp
        import numpy as np
        HEAD = 8
        BLOCK = 64
        D_MODEL = 128
        B, S, D = src.shape
        H, bs = (HEAD, BLOCK)
        dk = D // H
        nb = S // bs
        q = (src @ Wq + bq).reshape(B, nb, bs, H, dk)
        k = (src @ Wk + bk).reshape(B, nb, bs, H, dk)
        v = (src @ Wv + bv).reshape(B, nb, bs, H, dk)
        scores = jnp.einsum('bnqhd,bnkhd->bhnqk', q, k) * dk ** (-0.5)
        probs = jax.nn.softmax(scores, axis=-1)
        out = jnp.einsum('bhnqk,bnkhd->bnqhd', probs, v).reshape(B, S, D)
        return out @ Wo + bo

    def _L0_xattn_ref(q, k, v, mask, Wq, Wk, Wv, Wo):
        import jax, jax.numpy as jnp
        import numpy as np
        HIDDEN = 128
        HEADS = 16
        D_K = HIDDEN // HEADS
        SCALE = D_K ** (-0.5)
        B, S = (2, 256)
        b = q.shape[0]
        qh = (q @ Wq.T).reshape(b, -1, HEADS, D_K).transpose(0, 2, 1, 3)
        kh = (k @ Wk.T).reshape(b, -1, HEADS, D_K).transpose(0, 2, 1, 3)
        vh = (v @ Wv.T).reshape(b, -1, HEADS, D_K).transpose(0, 2, 1, 3)
        scores = jnp.einsum('bhqd,bhkd->bhqk', qh * SCALE, kh)
        scores = jnp.where(mask[:, None, :, :], jnp.float32(-1000000000.0), scores)
        attn = jax.nn.softmax(scores, axis=-1)
        out = jnp.einsum('bhqk,bhkd->bhqd', attn, vh)
        out = out.transpose(0, 2, 1, 3).reshape(b, -1, HEADS * D_K)
        return out @ Wo.T

    def _L0_ffn_ref(x, W1, W2, Wr):
        import jax, jax.numpy as jnp
        import numpy as np
        B, T, D = (2, 256, 128)
        E, DFF, TOPK = (8, 512, 2)
        TEMPERATURE = 1.0
        logits = jnp.einsum('btd,ed->bte', x, Wr)
        probs = jax.nn.softmax(logits / TEMPERATURE, axis=-1)
        topk_vals, topk_idx = jax.lax.top_k(probs, TOPK)
        router_weights = topk_vals / topk_vals.sum(-1, keepdims=True)
        one_hot = jax.nn.one_hot(topk_idx, E, dtype=x.dtype)
        gate = jnp.einsum('btk,btke->bte', router_weights, one_hot)
        h = jax.nn.silu(jnp.einsum('btd,efd->btef', x, W1))
        y = jnp.einsum('btef,edf->bted', h, W2)
        out = jnp.einsum('bte,bted->btd', gate, y)
        return out
    x = _layernorm(x + _L0_attn_ref(x, L0_attn_Wq, L0_attn_bq, L0_attn_Wk, L0_attn_bk, L0_attn_Wv, L0_attn_bv, L0_attn_Wo, L0_attn_bo), axis=-1)
    x = _layernorm(x + _L0_xattn_ref(x, ctx_1024, ctx_1024, mask_BxSxS2_bf0, L0_xattn_Wq, L0_xattn_Wk, L0_xattn_Wv, L0_xattn_Wo), axis=-1)
    x = _layernorm(x + _L0_ffn_ref(x, L0_ffn_W1, L0_ffn_W2, L0_ffn_Wr), axis=-1)
    return x

_drawn_inputs = setup_inputs


def setup_inputs(seed=0):
    import zlib

    import numpy as np

    out = dict(_drawn_inputs(seed))
    spreads = {}
    factors = {'L0_attn_Wq': 8.0,
     'L0_attn_bq': 8.0,
     'L0_attn_Wk': 8.0,
     'L0_attn_bk': 8.0,
     'L0_attn_Wv': 8.0,
     'L0_attn_bv': 8.0,
     'L0_attn_Wo': 7.45,
     'L0_attn_bo': 2.921}
    for name, (base, spread) in spreads.items():
        noise = np.random.default_rng([zlib.crc32(name.encode()), seed]).standard_normal(out[name].shape)
        drawn = base * np.exp(spread * noise) if base else spread * noise
        out[name] = jnp.asarray(drawn.astype(out[name].dtype))
    for name, factor in factors.items():
        out[name] = (out[name] * factor).astype(out[name].dtype)
    return out
```

```python
import numpy as np
import concourse.bass as bass
from concourse import mybir
from contextlib import ExitStack

F32, F16, BF16, U8, U32 = (mybir.dt.float32, mybir.dt.float16, mybir.dt.bfloat16, mybir.dt.uint8, mybir.dt.uint32)
ACT = mybir.ActivationFunctionType
ALU = mybir.AluOpType
AX = mybir.AxisListType

B, S, D = 128, 64, 128
TOK = B * S
P = 128
NT = TOK // P
GT = 4
GTOK = GT * P
G = NT // GT
GB = GTOK // S
HB = GB // 2
E, DFF, FC = 8, 512, 4
EPS = 1e-5
WS = 64.0
IWS = 1.0 / WS
BIG = float(2.0 ** 100)


class Layer:
    def __init__(self, name, heads, cross, w):
        self.name, self.cross = name, cross
        self.dk = D // heads
        self.quads = heads // 4
        self.rows = D // self.quads
        self.nh = self.quads * 2
        self.wq, self.wk, self.wv, self.wo = w
        self.qscale = IWS * float(np.float32(self.dk ** -0.5))


SELF = Layer("self", 8, False, (0, 1, 2, 3))
CROSS = Layer("cross", 16, True, (4, 5, 6, 7))


def wait(eng, sem, value):
    if isinstance(value, int) and value <= 0:
        return
    eng.wait_ge(sem, value)


def wait_apart(eng, sem, value, reached, count):
    value = value if isinstance(value, int) else eng.to_reg(value)
    eng.wait_ge(reached, count)
    wait(eng, sem, value)


def units(layer):
    return [(u // 2, u % 2) for u in range(layer.nh)]


def program(nc, x, ctx_in, mask, wstack, biases, w1, w2, wr, const, out):
    ctx = ExitStack()
    with ctx:
        def sb(name, shape, dt):
            return ctx.enter_context(nc.sbuf_tensor(name, shape, dt))

        def sem(name):
            return ctx.enter_context(nc.semaphore(name))

        X = sb("X", [P, NT, D], F32)
        ident = sb("ident", [P, P], F32)
        cst = sb("cst", [P, 16], F32)
        Wf = sb("Wf", [P, 8, D], F32)
        Wh = sb("Wh", [P, 8, D], F16)
        Wl = sb("Wl", [P, 8, D], F16)
        Wrf = sb("Wrf", [P, E], F32)
        Wrh = sb("Wrh", [P, E], F16)
        Wrl = sb("Wrl", [P, E], F16)
        bf = sb("bf", [2, 4 * D], F32)
        bh = sb("bh", [2, 4 * D], F16)
        bl = sb("bl", [2, 4 * D], F32)
        b2 = sb("b2", [2, 4 * D], F16)
        ones2 = sb("ones2", [2, GTOK], F16)
        negI = sb("negI", [S, 2 * S], BF16)
        W1h = sb("W1h", [P, E * DFF], F16)
        W1l = sb("W1l", [P, E * DFF], F16)
        W2h = sb("W2h", [P, E * DFF], F16)
        W2l = sb("W2l", [P, E * DFF], F16)
        wst = sb("wst", [P, E * DFF], F32)
        xth = [sb(f"xth{i}", [P, GTOK], F16) for i in range(2)]
        xtl = [sb(f"xtl{i}", [P, GTOK], F16) for i in range(2)]
        cin = [sb(f"cin{i}", [P, GT, D], F32) for i in range(2)]
        cth = [sb(f"cth{i}", [P, GTOK], F16) for i in range(2)]
        ctl = [sb(f"ctl{i}", [P, GTOK], F16) for i in range(2)]
        mraw = [sb(f"mraw{i}", [S, GB, S], U8) for i in range(2)]
        mbf = [sb(f"mbf{i}", [S, GB, S], BF16) for i in range(2)]
        qh = sb("qh", [P, GTOK], F16)
        ql = sb("ql", [P, GTOK], F16)
        qzh = [sb(f"qzh{i}", [P, GB, 4, S], F16) for i in range(2)]
        qzl = [sb(f"qzl{i}", [P, GB, 4, S], F16) for i in range(2)]
        kh = [sb(f"kh{i}", [P, GTOK], F16) for i in range(2)]
        kl = [sb(f"kl{i}", [P, GTOK], F16) for i in range(2)]
        vz = {}
        for la in (SELF, CROSS):
            for part in "hl":
                vz[la.name, part] = [sb(f"vz_{la.name}_{part}{i}", [P, 2, GT * la.quads, 2, 2, la.dk + 1], F16)
                                     for i in range(2)]
        pr = [sb(f"pr{i}", [P, 512], F32) for i in range(2)]
        pth = [sb(f"pth{i}", [P, 512], F16) for i in range(2)]
        ptl = [sb(f"ptl{i}", [P, 512], F16) for i in range(2)]
        mx = [sb(f"mx{i}", [P, 8], F32) for i in range(2)]
        rc = [sb(f"rc{i}", [P, HB, 4], F32) for i in range(2)]
        at = [sb(f"at{i}", [P, GT, D], F32) for i in range(2)]
        ath = sb("ath", [P, GTOK], F16)
        atl = sb("atl", [P, GTOK], F16)
        xs = [sb(f"xs{i}", [P, GT, D], F32) for i in range(2)]
        z = sb("z", [P, GT, D], F32)
        z2 = sb("z2", [P, GT, D], F32)
        st = sb("st", [P, GT, 6], F32)
        mv = sb("mv", [P, GT, 2], F32)
        ve = sb("ve", [P, GT], F32)
        mhalf = sb("mhalf", [P, GT], F32)
        rstd = sb("rstd", [P, GT], F32)
        XTh = sb("XTh", [P, TOK], F16)
        XTl = sb("XTl", [P, TOK], F16)
        lg, prob, hot0, hot1 = (wst[:, n * NT * E:(n + 1) * NT * E].rearrange("p (t e) -> p t e", e=E) for n in range(4))
        hot = (hot0, hot1)
        rt = wst[:, 4 * NT * E:4 * NT * E + 7 * NT].rearrange("p (r t) -> p r t", t=NT)
        gate = sb("gate", [P, G, E, GT], F32)
        s32 = pr + [xs[i][:].rearrange("p t d -> p (t d)") for i in range(2)]
        sh = pth + xth
        sl = ptl + xtl

        bank = [ctx.enter_context(nc.psum_tensor(f"bank{i}", [P, 512], F32)) for i in range(8)]
        SC, TB, PVB, M0, M1 = bank[0:2], bank[2:4], bank[4:6], bank[6], bank[7]

        ld_x = [sem("ld_x0"), sem("ld_x1")]
        ld_w, ld_w1, ld_w2 = sem("ld_w"), sem("ld_w1"), sem("ld_w2")
        pool_ready, prep, wh_done, w1_split, w2_split = (sem(n) for n in "pool_ready prep wh_done w1_split w2_split".split())
        var_eps = sem("var_eps")
        ld_c = [sem("ld_c0"), sem("ld_c1")]
        ld_m = [sem("ld_m0"), sem("ld_m1")]
        mask_done = sem("mask_done")
        NAMES = ("xs xt xh xl ct ch cl q qh ql qz k kh kl v vh vl s mx sub ex t ph pl pv rc nm at ah al o zz st mv rs fin").split()
        sems = {la.name: {n: sem(f"{la.name}_{n}") for n in NAMES} for la in (SELF, CROSS)}
        r_xt, r_xh, r_xl, r_lg, r_lc = sem("r_xt"), sem("r_xh"), sem("r_xl"), sem("r_lg"), sem("r_lc")
        r_xs, r_sub, r_ex = sem("r_xs"), sem("r_sub"), sem("r_ex")
        f_h, f_si, f_sh, f_sl, f_y, f_ac, f_st, f_mv, f_rs, f_fin, stored = (sem(n) for n in (
            "f_h f_si f_sh f_sl f_y f_ac f_st f_mv f_rs f_fin stored").split())

        block = ctx.enter_context(nc.Block())
        x_v = x.rearrange("b s d -> (b s) d").rearrange("(g t p) d -> g p t d", t=GT, p=P)
        c_v = ctx_in.rearrange("b s d -> (b s) d").rearrange("(g t p) d -> g p t d", t=GT, p=P)
        o_v = out.rearrange("b s d -> (b s) d").rearrange("(g t p) d -> g p t d", t=GT, p=P)
        m_v = mask.rearrange("(g b) q k -> g q b k", b=GB)

        def over_groups(eng, body):
            body(0, 0, True, False)
            with eng.Fori(0, (G - 2) // 2) as j:
                body(2 * j + 1, 1, False, False)
                body(2 * j + 2, 0, False, False)
            body(G - 1, 1, False, True)

        def expert_loop(eng, expert):
            def rest(g):
                with eng.Fori(1, E // 2) as j:
                    expert(g, 2 * j, 0, False, False)
                    expert(g, 2 * j + 1, 1, False, False)
            expert(0, 0, 0, True, True)
            expert(0, 1, 1, False, False)
            rest(0)
            with eng.Fori(1, G) as g:
                expert(g, 0, 0, False, True)
                expert(g, 1, 1, False, False)
                rest(g)

        def vsrc(la, b2_, jp):
            return M0[S * b2_:S * b2_ + S, :].rearrange("p (n j c d) -> p n j c d", j=2, c=2, d=la.dk)[:, :, jp]

        def vdst(la, part, i, b2_, jp):
            return vz[la.name, part][i][S * jp:S * jp + S, b2_, :, jp, :, 0:la.dk]

        @block.sync
        def _(sp):
            sp.dma_start(ident[:], const[:, 0:P]).then_inc(ld_w, 16)
            sp.dma_start(cst[:], const[:, P:P + 16]).then_inc(ld_w, 16)
            sp.dma_start(Wf[:], wstack.rearrange("w p d -> p w d")).then_inc(ld_w, 16)
            sp.dma_start(Wrf[:], wr).then_inc(ld_w, 16)
            sp.dma_start(bf[0:1, :], biases).then_inc(ld_w, 16)
            sp.dma_start(bf[1:2, :], biases).then_inc(ld_w, 16)
            for g in range(2):
                sp.dma_start(X[:, g * GT:(g + 1) * GT, :], x_v[g]).then_inc(ld_x[g], 16)
            with sp.Fori(1, G // 2) as j:
                for i in range(2):
                    wait_apart(sp, ld_x[i], 16 * j, ld_x[i], 16)
                    sp.dma_start(X[:, bass.ds((2 * j + i) * GT, GT), :], x_v[bass.ds(2 * j + i, 1)].rearrange("o p t d -> p (o t) d")).then_inc(ld_x[i], 16)
            sp.dma_start(wst[:], w1).then_inc(ld_w1, 16)
            for g in range(2):
                sp.dma_start(cin[g][:], c_v[g]).then_inc(ld_c[g], 16)
                sp.dma_start(mraw[g][:], m_v[g]).then_inc(ld_m[g], 16)
            sp.wait_ge(w1_split, 2)
            sp.dma_start(wst[:], w2).then_inc(ld_w2, 16)
            sc = sems["cross"]
            with sp.Fori(1, G // 2) as j:
                for i in range(2):
                    wait_apart(sp, sc["ct"], 2 * j + i - 1, ld_x[i], 16)
                    sp.dma_start(cin[i][:], c_v[bass.ds(2 * j + i, 1)].rearrange("o p t d -> p (o t) d")).then_inc(ld_c[i], 16)
                    wait_apart(sp, mask_done, 2 * j + i - 1, ld_x[i], 16)
                    sp.dma_start(mraw[i][:], m_v[bass.ds(2 * j + i, 1)].rearrange("o q b k -> q (o b) k")).then_inc(ld_m[i], 16)
            with sp.Fori(0, G) as g:
                wait_apart(sp, f_fin, g + 1, ld_x[0], 16)
                sp.dma_start(o_v[bass.ds(g, 1)].rearrange("o p t d -> p (o t) d"), z[:]).then_inc(stored, 16)
            sp.wait_ge(stored, 16 * G)

        @block.gpsimd
        def _(pool):
            nc.gpsimd.memset(ones2[:], 1.0).then_inc(pool_ready, 1)
            nc.gpsimd.memset(mhalf[:], -0.5).then_inc(pool_ready, 1)
            zeroed = [nc.gpsimd.memset(v[:].rearrange("p a b c d e -> p (a b c d e)"), 0.0).then_inc(pool_ready, 1)
                      for pair in vz.values() for v in pair]
            pool.wait_ge(pool_ready, 2 + len(zeroed))
            for la in (SELF, CROSS):
                for v in vz[la.name, "h"]:
                    for jp in range(2):
                        for par in range(2):
                            nc.gpsimd.memset(v[S * jp:S * jp + S, par, :, jp, :, la.dk:la.dk + 1], WS).then_inc(pool_ready, 1)

            def stage(g, i, done, transposed):
                wait_apart(pool, transposed, g - 1, pool_ready, POOL_READY)
                nc.gpsimd.tensor_copy(xs[i][:], X[:, bass.ds(g * GT, GT), :]).then_inc(done, 1)

            def inv_std(g, stats_done, before, done):
                wait_apart(pool, stats_done, g + 1, pool_ready, POOL_READY)
                nc.gpsimd.tensor_scalar(ve[:], mv[:, :, 1], EPS, None, ALU.add).then_inc(var_eps, 1)
                pool.wait_ge(var_eps, before + g + 1)
                nc.gpsimd.tensor_tensor(rstd[:], ve[:], mhalf[:], ALU.pow).then_inc(done, 1)

            def convert(g, i):
                wait_apart(pool, ld_m[i], 8 * (g - i) + 16, pool_ready, POOL_READY)
                wait_apart(pool, sems["cross"]["s"], (g - 1) * CROSS.nh, pool_ready, POOL_READY)
                nc.gpsimd.tensor_copy(mbf[i][:], mraw[i][:]).then_inc(mask_done, 1)

            def attention(la, before):
                s = sems[la.name]

                def ahead(g, i):
                    if not la.cross:
                        wait_apart(pool, ld_x[i], 8 * (g - i) + 16, pool_ready, POOL_READY)
                    stage(g, i, s["xs"], s["xt"])
                    if la.cross:
                        convert(g, i)

                def body(g, i, first, last):
                    if not last:
                        ahead(g + 1, 1 - i)
                    if not first:
                        inv_std(g - 1, s["mv"], before, s["rs"])
                ahead(0, 0)
                over_groups(pool, body)
                inv_std(G - 1, s["mv"], before, s["rs"])

            pool.wait_ge(pool_ready, POOL_READY)
            attention(SELF, 0)
            pool.wait_ge(sems["self"]["fin"], G)
            attention(CROSS, G)
            pool.wait_ge(sems["cross"]["fin"], G)
            with pool.Fori(0, G // 2) as j:
                for i in range(2):
                    wait_apart(pool, r_xt, 2 * j + i, pool_ready, POOL_READY)
                    nc.gpsimd.tensor_copy(xs[i][:], X[:, bass.ds((2 * j + i) * GT, GT), :]).then_inc(r_xs, 1)

            def expert(g, e, par, first, head):
                for f in range(FC):
                    n = g * (E * FC) + e * FC + f
                    wait_apart(pool, f_si, n + 1, pool_ready, POOL_READY)
                    nc.gpsimd.tensor_copy(sh[f][:], s32[f][:]).then_inc(f_sh, 1)
                    if head and not first and f == 2:
                        inv_std(g - 1, f_mv, 2 * G, f_rs)
            expert_loop(pool, expert)
            inv_std(G - 1, f_mv, 2 * G, f_rs)

        @block.tensor
        def _(pe):
            def three(out_, l, r, start=True, stop=True, last_inc=None, **kw):
                (lh, ll), (rh, rl) = l, r
                nc.tensor.matmul(out_, lh, rh, start=start, stop=False, **kw)
                nc.tensor.matmul(out_, lh, rl, start=False, stop=False, **kw)
                return nc.tensor.matmul(out_, ll, rh, start=False, stop=stop, **kw)

            def attention(la):
                s = sems[la.name]
                us = units(la)
                R, W = la.rows, 4 * (la.dk + 1)

                def XT(g, i):
                    pe.wait_ge(s["xs"], g + 1)
                    wait(pe, s["vl"], g)
                    for t in range(GT):
                        m = nc.tensor.transpose(M0[:, t * P:(t + 1) * P], xs[i][:, t, :], ident[:])
                    m.then_inc(s["xt"], 1)

                def CT(g, i):
                    pe.wait_ge(ld_c[i], 8 * (g - i) + 16)
                    wait(pe, s["zz"], g - 2)
                    for t in range(GT):
                        m = nc.tensor.transpose(M1[:, t * P:(t + 1) * P], cin[i][:, t, :], ident[:])
                    m.then_inc(s["ct"], 1)

                def proj(out_, w, r, bias, done):
                    m = three(out_, (Wh[:, w, :], Wl[:, w, :]), r, stop=bias is None)
                    if bias is not None:
                        m = nc.tensor.matmul(out_, b2[:, bias * D:(bias + 1) * D], ones2[:], start=False, stop=True)
                    m.then_inc(done, 1)

                def Qp(g, i):
                    pe.wait_ge(s["xl"], g + 1)
                    proj(M0[:], la.wq, (xth[i][:], xtl[i][:]), None if la.cross else 0, s["q"])

                def Kp(g, i):
                    if la.cross:
                        pe.wait_ge(s["cl"], g + 1)
                        proj(M1[:], la.wk, (cth[i][:], ctl[i][:]), None, s["k"])
                    else:
                        wait(pe, s["zz"], g - 2)
                        proj(M1[:], la.wk, (xth[i][:], xtl[i][:]), 1, s["k"])

                def Vp(g, i):
                    pe.wait_ge(s["ql"], g + 1)
                    src = (cth[i], ctl[i]) if la.cross else (xth[i], xtl[i])
                    for t in range(GT):
                        c = slice(t * P, (t + 1) * P)
                        m = three(M0[:, c], (src[0][:, c], src[1][:, c]), (Wh[:, la.wv, :], Wl[:, la.wv, :]), stop=la.cross)
                        if not la.cross:
                            m = nc.tensor.matmul(M0[:, c], ones2[:, 0:P], b2[:, 2 * D:3 * D], start=False, stop=True)
                    m.then_inc(s["v"], 1)

                def scores(g, u, i):
                    n = g * la.nh + u
                    quad, half = us[u]
                    wait(pe, s["sub"], n - 1)
                    if u == 0:
                        pe.wait_ge(s["kl"], g + 1)
                    r = slice(quad * R, (quad + 1) * R)
                    bnk = SC[u % 2]
                    if la.cross:
                        if u == 0:
                            pe.wait_ge(mask_done, g + 1)
                        nc.tensor.matmul(bnk[:].rearrange("p (b j k) -> p b j k", b=HB, j=2), negI[:],
                                         mbf[i][:, half * HB:(half + 1) * HB, :].unsqueeze(2).to_broadcast([S, HB, 2, S]),
                                         start=True, stop=False, skip_group_check=True)
                    for b in range(HB):
                        bb = half * HB + b
                        for jp in range(2):
                            o = bnk[:, b * P + jp * S:b * P + (jp + 1) * S]
                            lh, ll = (q[i][r, bb, 2 * jp:2 * jp + 2, :].rearrange("p c s -> p (c s)") for q in (qzh, qzl))
                            rh, rl = (k[i][r, bb * S:(bb + 1) * S] for k in (kh, kl))
                            m = three(o, (lh, ll), (rh, rl), start=not la.cross, skip_group_check=la.cross)
                    m.then_inc(s["s"], 1)

                def flip(g, u, i):
                    n = g * la.nh + u
                    pe.wait_ge(s["ex"], n + 1)
                    wait(pe, s["pl"], n - 1)
                    for b in range(HB):
                        m = nc.tensor.transpose(TB[u % 2][:, b * P:(b + 1) * P], pr[u % 2][:, b * P:(b + 1) * P], ident[:])
                    m.then_inc(s["t"], 1)

                def values(g, u, i):
                    n = g * la.nh + u
                    quad, half = us[u]
                    pe.wait_ge(s["pl"], n + 1)
                    wait(pe, s["nm"], n - 1)
                    if u == 0:
                        pe.wait_ge(s["vl"], g + 1)
                    for b in range(HB):
                        bb = half * HB + b
                        c = slice(b * P, (b + 1) * P)
                        v = [vz[la.name, part][i][:, bb % 2, (bb // 2) * la.quads + quad].rearrange("p j c d -> p (j c d)") for part in "hl"]
                        m = three(PVB[u % 2][:, b * W:(b + 1) * W], (pth[u % 2][:, c], ptl[u % 2][:, c]), v)
                    m.then_inc(s["pv"], 1)

                def AT(g, i):
                    pe.wait_ge(s["nm"], (g + 1) * la.nh)
                    pe.wait_ge(s["kl"], min(g + 3, G) if isinstance(g, int) else g + 3)
                    for t in range(GT):
                        m = nc.tensor.transpose(M1[:, t * P:(t + 1) * P], at[i][:, t, :], ident[:])
                    m.then_inc(s["at"], 1)

                def O(g, i):
                    pe.wait_ge(s["al"], g + 1)
                    for t in range(GT):
                        c = slice(t * P, (t + 1) * P)
                        m = three(M1[:, c], (ath[:, c], atl[:, c]), (Wh[:, la.wo, :], Wl[:, la.wo, :]), stop=la.cross)
                        if not la.cross:
                            m = nc.tensor.matmul(M1[:, c], ones2[:, 0:P], b2[:, 3 * D:4 * D], start=False, stop=True)
                    m.then_inc(s["o"], 1)

                def body(g, i, first, last):
                    for u in range(la.nh):
                        if u == slot(la, "O") and not first:
                            O(g - 1, 1 - i)
                        if u + 1 < la.nh:
                            scores(g, u + 1, i)
                        elif not last:
                            scores(g + 1, 0, 1 - i)
                        flip(g, u, i)
                        if u > 0:
                            values(g, u - 1, i)
                        elif not first:
                            values(g - 1, la.nh - 1, 1 - i)
                        if not last:
                            if u == slot(la, "XT"):
                                XT(g + 1, 1 - i)
                            if la.cross and u == slot(la, "CT"):
                                CT(g + 1, 1 - i)
                            if u == slot(la, "QK"):
                                Qp(g + 1, 1 - i)
                                Kp(g + 1, 1 - i)
                            if u == slot(la, "V"):
                                Vp(g + 1, 1 - i)
                        if u == slot(la, "AT") and not first:
                            AT(g - 1, 1 - i)

                XT(0, 0)
                if la.cross:
                    CT(0, 0)
                Qp(0, 0)
                Kp(0, 0)
                Vp(0, 0)
                scores(0, 0, 0)
                over_groups(pe, body)
                values(G - 1, la.nh - 1, 1)
                AT(G - 1, 1)
                O(G - 1, 1)

            pe.wait_ge(prep, PREP)
            attention(SELF)
            pe.wait_ge(sems["self"]["fin"], G)
            attention(CROSS)

            pe.wait_ge(sems["cross"]["fin"], G)
            pe.wait_ge(prep, PREP)

            def route(g, i):
                tb, lb = bank[i], bank[2 + i]
                pe.wait_ge(r_xs, g + 1)
                for t in range(GT):
                    m = nc.tensor.transpose(tb[:, t * P:(t + 1) * P], xs[i][:, t, :], ident[:])
                m.then_inc(r_xt, 1)
                pe.wait_ge(r_xl, g + 1)
                for t in range(GT):
                    rows = [q[:, bass.ds(g * GTOK + t * P, P)] for q in (XTh, XTl)]
                    m = three(lb[:, t * E:(t + 1) * E], rows, (Wrh[:], Wrl[:]))
                m.then_inc(r_lg, 1)
                pe.wait_ge(r_lc, g + 1)
            with pe.Fori(0, G // 2) as j:
                route(2 * j, 0)
                route(2 * j + 1, 1)

            H, Y = bank[0:4], bank[4:6]

            def up(g, e, f):
                n = g * (E * FC) + e * FC + f
                wait(pe, f_si, n - 3)
                cols = bass.ds(e * DFF + f * P, P)
                rows = [q[:, bass.ds(g * GTOK, GTOK)] for q in (XTh, XTl)]
                three(H[f][:], (W1h[:, cols], W1l[:, cols]), rows).then_inc(f_h, 1)

            def down(g, e, f, par):
                n = g * (E * FC) + e * FC + f
                pe.wait_ge(f_sl, n + 1)
                if f == 0:
                    wait(pe, f_ac, g * E + e - 1)
                cols = bass.ds((e * FC + f) * D, D)
                for t in range(GT):
                    c = slice(t * P, (t + 1) * P)
                    m = three(Y[par][:, c], (sh[f][:, c], sl[f][:, c]), (W2h[:, cols], W2l[:, cols]),
                              start=(f == 0 and t == 0), stop=(f == FC - 1), skip_group_check=True)
                if f == FC - 1:
                    m.then_inc(f_y, 1)

            def expert(g, e, par, first, head):
                for f in range(FC):
                    up(g, e, f)
                    if f >= 2:
                        down(g, e, f - 2, par)
                    elif head and not first:
                        down(g - 1, E - 1, f + 2, 1 - par)
                    elif not first:
                        down(g, e - 1, f + 2, 1 - par)

            pe.wait_ge(w1_split, 2)
            pe.wait_ge(w2_split, 2)
            expert_loop(pe, expert)
            down(G - 1, E - 1, 2, 1)
            down(G - 1, E - 1, 3, 1)

        @block.scalar
        def _(act):
            act.wait_ge(ld_w, 96)
            nc.scalar.activation(Wh[:], Wf[:], ACT.Copy, scale=WS).then_inc(wh_done, 1)

            def attention(la):
                s = sems[la.name]
                us = units(la)

                def xh(g, i):
                    act.wait_ge(s["xt"], g + 1)
                    nc.scalar.activation(xth[i][:], M0[:], ACT.Copy).then_inc(s["xh"], 1)

                def ch(g, i):
                    act.wait_ge(s["ct"], g + 1)
                    nc.scalar.activation(cth[i][:], M1[:], ACT.Copy).then_inc(s["ch"], 1)

                def qkh(g, i):
                    act.wait_ge(s["q"], g + 1)
                    nc.scalar.activation(qh[:], M0[:], ACT.Copy, scale=la.qscale).then_inc(s["qh"], 1)
                    act.wait_ge(s["k"], g + 1)
                    nc.scalar.activation(kh[i][:], M1[:], ACT.Copy, scale=IWS).then_inc(s["kh"], 1)

                def vh(g, i):
                    act.wait_ge(s["v"], g + 1)
                    for b2_ in range(2):
                        for jp in range(2):
                            m = nc.scalar.activation(vdst(la, "h", i, b2_, jp), vsrc(la, b2_, jp), ACT.Copy)
                    m.then_inc(s["vh"], 1)

                def ex(g, u):
                    act.wait_ge(s["sub"], g * la.nh + u + 1)
                    nc.scalar.activation(pr[u % 2][:], pr[u % 2][:], ACT.Exp).then_inc(s["ex"], 1)

                def ph(g, u):
                    act.wait_ge(s["t"], g * la.nh + u + 1)
                    nc.scalar.activation(pth[u % 2][:], TB[u % 2][:], ACT.Copy).then_inc(s["ph"], 1)

                def ah(g):
                    act.wait_ge(s["at"], g + 1)
                    nc.scalar.activation(ath[:], M1[:], ACT.Copy).then_inc(s["ah"], 1)

                def body(g, i, first, last):
                    for u in range(la.nh):
                        ph(g, u)
                        if u + 1 < la.nh:
                            ex(g, u + 1)
                        elif not last:
                            ex(g + 1, 0)
                        if not last:
                            if u == slot(la, "XT"):
                                xh(g + 1, 1 - i)
                            if la.cross and u == slot(la, "CT"):
                                ch(g + 1, 1 - i)
                            if u == slot(la, "QK"):
                                qkh(g + 1, 1 - i)
                            if u == slot(la, "V"):
                                vh(g + 1, 1 - i)
                        if u == slot(la, "AT") and not first:
                            ah(g - 1)

                xh(0, 0)
                if la.cross:
                    ch(0, 0)
                qkh(0, 0)
                vh(0, 0)
                ex(0, 0)
                over_groups(act, body)
                ah(G - 1)

            act.wait_ge(pool_ready, POOL_READY)
            attention(SELF)
            attention(CROSS)

            def route(g, i):
                act.wait_ge(r_xt, g + 1)
                nc.scalar.activation(XTh[:, bass.ds(g * GTOK, GTOK)], bank[i][:], ACT.Copy).then_inc(r_xh, 1)
            with act.Fori(0, G // 2) as j:
                route(2 * j, 0)
                route(2 * j + 1, 1)
            act.wait_ge(r_sub, 1)
            nc.scalar.activation(prob, lg, ACT.Exp).then_inc(r_ex, 1)

            def silu(g, e, f):
                n = g * (E * FC) + e * FC + f
                act.wait_ge(f_h, n + 1)
                wait(act, f_sl, n - 3)
                nc.scalar.activation(s32[f][:], bank[f][:], ACT.Silu, scale=IWS).then_inc(f_si, 1)

            def expert(g, e, par, first, head):
                for f in range(FC):
                    silu(g, e, f)
            expert_loop(act, expert)

        @block.vector
        def _(dve):
            links = [0]

            def link(ins):
                links[0] += 1
                ins.then_inc(prep, 1)
                dve.wait_ge(prep, links[0])

            dve.wait_ge(ld_w, 96)
            dve.wait_ge(pool_ready, POOL_READY)
            dve.wait_ge(wh_done, 1)
            link(nc.vector.scalar_tensor_tensor(out=Wl[:], in0=Wf[:], scalar=WS, in1=Wh[:], op0=ALU.mult, op1=ALU.subtract))
            link(nc.vector.tensor_scalar(Wrh[:], Wrf[:], WS, None, ALU.mult))
            link(nc.vector.scalar_tensor_tensor(out=Wrl[:], in0=Wrf[:], scalar=WS, in1=Wrh[:], op0=ALU.mult, op1=ALU.subtract))
            link(nc.vector.tensor_scalar(negI[:, 0:S], ident[0:S, 0:S], -BIG, None, ALU.mult))
            link(nc.vector.tensor_scalar(negI[:, S:2 * S], ident[0:S, 0:S], -BIG, None, ALU.mult))
            link(nc.vector.tensor_scalar(bh[:], bf[:], WS, None, ALU.mult))
            link(nc.vector.scalar_tensor_tensor(out=bl[:], in0=bf[:], scalar=WS, in1=bh[:], op0=ALU.mult, op1=ALU.subtract))
            link(nc.vector.tensor_scalar(bf[:], bl[:], ident[0:2, 1:2], None, ALU.mult))
            link(nc.vector.scalar_tensor_tensor(out=b2[:], in0=bh[:], scalar=ident[0:2, 0:1], in1=bf[:], op0=ALU.mult, op1=ALU.add))
            assert links[0] == PREP

            def split_w(dst_h, dst_l, ready, done):
                dve.wait_ge(ready, 16)
                nc.vector.tensor_scalar(dst_h[:], wst[:], WS, None, ALU.mult).then_inc(done, 1)
                dve.wait_ge(done, 1)
                nc.vector.scalar_tensor_tensor(out=dst_l[:], in0=wst[:], scalar=WS, in1=dst_h[:], op0=ALU.mult, op1=ALU.subtract).then_inc(done, 1)

            def attention(la):
                s = sems[la.name]
                us = units(la)
                W = 4 * (la.dk + 1)
                hm = cst[:, 4:8] if la.cross else cst[:, 0:4]

                def low(dst, psum, high, scale, done):
                    nc.vector.scalar_tensor_tensor(out=dst, in0=psum, scalar=scale, in1=high, op0=ALU.mult, op1=ALU.subtract).then_inc(done, 1)

                def xl(g, i):
                    dve.wait_ge(s["xh"], g + 1)
                    nc.vector.tensor_tensor(xtl[i][:], M0[:], xth[i][:], ALU.subtract).then_inc(s["xl"], 1)

                def cl(g, i):
                    dve.wait_ge(s["ch"], g + 1)
                    nc.vector.tensor_tensor(ctl[i][:], M1[:], cth[i][:], ALU.subtract).then_inc(s["cl"], 1)

                def qkl(g, i):
                    dve.wait_ge(s["qh"], g + 1)
                    low(ql[:], M0[:], qh[:], la.qscale, s["ql"])
                    for hc in range(4):
                        nc.vector.tensor_scalar(qzh[i][:, :, hc, :], qh[:].rearrange("p (b s) -> p b s", b=GB), hm[:, hc:hc + 1], None, ALU.mult)
                    dve.wait_ge(s["ql"], g + 1)
                    for hc in range(4):
                        m = nc.vector.tensor_scalar(qzl[i][:, :, hc, :], ql[:].rearrange("p (b s) -> p b s", b=GB), hm[:, hc:hc + 1], None, ALU.mult)
                    m.then_inc(s["qz"], 1)
                    dve.wait_ge(s["kh"], g + 1)
                    low(kl[i][:], M1[:], kh[i][:], IWS, s["kl"])

                def vl(g, i):
                    dve.wait_ge(s["vh"], g + 1)
                    for b2_ in range(2):
                        for jp in range(2):
                            m = nc.vector.tensor_tensor(vdst(la, "l", i, b2_, jp), vsrc(la, b2_, jp), vdst(la, "h", i, b2_, jp), ALU.subtract)
                    m.then_inc(s["vl"], 1)

                def soft(g, u):
                    n = g * la.nh + u
                    dve.wait_ge(s["s"], n + 1)
                    sc = SC[u % 2][:].rearrange("p (r k) -> p r k", k=S)
                    nc.vector.tensor_reduce(mx[u % 2][:], sc, AX.X, ALU.max).then_inc(s["mx"], 1)
                    dve.wait_ge(s["mx"], n + 1)
                    nc.vector.tensor_tensor(pr[u % 2][:].rearrange("p (r k) -> p r k", k=S), sc,
                                            mx[u % 2][:].unsqueeze(2).to_broadcast([P, 8, S]), ALU.subtract).then_inc(s["sub"], 1)

                def pl(g, u):
                    dve.wait_ge(s["ph"], g * la.nh + u + 1)
                    nc.vector.tensor_tensor(ptl[u % 2][:], TB[u % 2][:], pth[u % 2][:], ALU.subtract).then_inc(s["pl"], 1)

                def norm(g, u, i):
                    n = g * la.nh + u
                    quad, half = us[u]
                    dve.wait_ge(s["pv"], n + 1)
                    pv = PVB[u % 2][:, 0:HB * W].rearrange("p (b jc e) -> p b jc e", b=HB, jc=4)
                    nc.vector.reciprocal(rc[u % 2][:], pv[:, :, :, la.dk]).then_inc(s["rc"], 1)
                    dve.wait_ge(s["rc"], n + 1)
                    for c in range(2):
                        for b2_ in range(2):
                            rows = slice(S * c, S * c + S)
                            src = PVB[u % 2][rows, 0:HB * W].rearrange("p (t b j c e) -> p t b j c e", t=HB // 2, b=2, j=2, c=2)[:, :, b2_, :, c, 0:la.dk]
                            r = rc[u % 2][rows].rearrange("p (t b) (j c) -> p t b j c", b=2, c=2)[:, :, b2_, :, c].unsqueeze(3).to_broadcast([S, HB // 2, 2, la.dk])
                            dst = at[i][S * b2_:S * b2_ + S, half * 2:half * 2 + 2, :].rearrange(
                                "p t (c n j e) -> p t c n j e", c=2, n=la.quads, j=2)[:, :, c, quad]
                            m = nc.vector.tensor_tensor(dst, src, r, ALU.mult)
                    m.then_inc(s["nm"], 1)

                def al(g):
                    dve.wait_ge(s["ah"], g + 1)
                    nc.vector.tensor_tensor(atl[:], M1[:], ath[:], ALU.subtract).then_inc(s["al"], 1)

                def xg(g):
                    return X[:, bass.ds(g * GT, GT), :]

                def stats(g):
                    dve.wait_ge(s["o"], g + 1)
                    nc.vector.scalar_tensor_tensor(out=z[:], in0=M1[:].rearrange("p (t d) -> p t d", t=GT), scalar=IWS, in1=xg(g),
                                                   op0=ALU.mult, op1=ALU.add).then_inc(s["zz"], 1)
                    dve.wait_ge(s["zz"], g + 1)
                    layer_stats(s["st"], s["mv"], g)

                def finish(g):
                    layer_norm(s["rs"], g, xg(g), s["fin"])

                def body(g, i, first, last):
                    for u in range(la.nh):
                        if u + 1 < la.nh:
                            soft(g, u + 1)
                        elif not last:
                            soft(g + 1, 0)
                        if u == slot(la, "O") and not first:
                            stats(g - 1)
                        pl(g, u)
                        if u > 0:
                            norm(g, u - 1, i)
                        elif not first:
                            norm(g - 1, la.nh - 1, 1 - i)
                        if not last:
                            if u == slot(la, "XT"):
                                xl(g + 1, 1 - i)
                            if la.cross and u == slot(la, "CT"):
                                cl(g + 1, 1 - i)
                            if u == slot(la, "QK"):
                                qkl(g + 1, 1 - i)
                            if u == slot(la, "V"):
                                vl(g + 1, 1 - i)
                        if u == slot(la, "AT") and not first:
                            al(g - 1)
                        if u == slot(la, "O") and not first:
                            finish(g - 1)

                xl(0, 0)
                if la.cross:
                    cl(0, 0)
                qkl(0, 0)
                vl(0, 0)
                soft(0, 0)
                over_groups(dve, body)
                norm(G - 1, la.nh - 1, 1)
                al(G - 1)
                stats(G - 1)
                finish(G - 1)

            def layer_stats(st_sem, mv_sem, g):
                for t in range(GT):
                    m = nc.vector.bn_stats(st[:, t, :], z[:, t, :])
                m.then_inc(st_sem, 1)
                wait_apart(dve, st_sem, g + 1, prep, PREP)
                for t in range(GT):
                    m = nc.vector.bn_aggr(mv[:, t, :], st[:, t, :])
                m.then_inc(mv_sem, 1)

            def layer_norm(rs_sem, g, dst, done):
                dve.wait_ge(rs_sem, g + 1)
                for t in range(GT):
                    m = nc.vector.tensor_scalar(dst[:, t, :], z[:, t, :], mv[:, t, 0:1], rstd[:, t:t + 1], ALU.subtract, ALU.mult)
                m.then_inc(done, 1)

            attention(SELF)
            split_w(W1h, W1l, ld_w1, w1_split)
            split_w(W2h, W2l, ld_w2, w2_split)
            attention(CROSS)

            def route(g, i):
                dve.wait_ge(r_xh, g + 1)
                cols = bass.ds(g * GTOK, GTOK)
                nc.vector.tensor_tensor(XTl[:, cols], bank[i][:], XTh[:, cols], ALU.subtract).then_inc(r_xl, 1)
                dve.wait_ge(r_lg, g + 1)
                nc.vector.tensor_scalar(lg[:, bass.ds(g * GT, GT), :], bank[2 + i][:, 0:GT * E].rearrange("p (t e) -> p t e", t=GT),
                                        IWS, None, ALU.mult).then_inc(r_lc, 1)
            with dve.Fori(0, G // 2) as j:
                route(2 * j, 0)
                route(2 * j + 1, 1)
            dve.wait_ge(r_lc, G)
            def each(v):
                return v.unsqueeze(2).to_broadcast([P, NT, E])

            link(nc.vector.tensor_reduce(rt[:, 0], lg, AX.X, ALU.max))
            nc.vector.tensor_tensor(lg, lg, each(rt[:, 0]), ALU.subtract).then_inc(r_sub, 1)
            dve.wait_ge(r_ex, 1)
            link(nc.vector.tensor_reduce(rt[:, 1], prob, AX.X, ALU.add))
            link(nc.vector.reciprocal(rt[:, 2], rt[:, 1]))
            link(nc.vector.tensor_tensor(prob, prob, each(rt[:, 2]), ALU.mult))
            rank = cst[:, 8:16].unsqueeze(1).to_broadcast([P, NT, E])
            for k in range(2):
                top, first = rt[:, 3 + k], rt[:, 5 + k]
                link(nc.vector.tensor_reduce(top, prob, AX.X, ALU.max))
                link(nc.vector.tensor_tensor(hot[k], prob, each(top), ALU.is_equal))
                link(nc.vector.tensor_tensor(hot[k], hot[k], rank, ALU.mult))
                link(nc.vector.tensor_reduce(first, hot[k], AX.X, ALU.min))
                link(nc.vector.tensor_tensor(hot[k], rank, each(first), ALU.is_equal))
                if k == 0:
                    link(nc.vector.scalar_tensor_tensor(out=prob, in0=hot[k], scalar=-2.0, in1=prob, op0=ALU.mult, op1=ALU.add))
            link(nc.vector.tensor_tensor(rt[:, 0], rt[:, 3], rt[:, 4], ALU.add))
            link(nc.vector.reciprocal(rt[:, 1], rt[:, 0]))
            for k in range(2):
                link(nc.vector.scalar_tensor_tensor(out=rt[:, 5 + k], in0=rt[:, 3 + k], scalar=IWS, in1=rt[:, 1], op0=ALU.mult, op1=ALU.mult))
                link(nc.vector.tensor_tensor(hot[k], hot[k], each(rt[:, 5 + k]), ALU.mult))
            link(nc.vector.tensor_tensor(gate[:].rearrange("p g e t -> p g t e"), hot[0].rearrange("p (g t) e -> p g t e", t=GT),
                                         hot[1].rearrange("p (g t) e -> p g t e", t=GT), ALU.add))

            def low(g, e, f):
                n = g * (E * FC) + e * FC + f
                dve.wait_ge(f_sh, n + 1)
                nc.vector.tensor_tensor(sl[f][:], s32[f][:], sh[f][:], ALU.subtract).then_inc(f_sl, 1)

            def add(g, e, par, fresh):
                m_ = g * E + e
                dve.wait_ge(f_y, m_ + 1)
                if not fresh:
                    dve.wait_ge(f_ac, m_)
                for t in range(GT):
                    base = X[:, bass.ds(g * GT + t, 1), :].rearrange("p o d -> p (o d)") if fresh else z2[:, t, :]
                    gcol = gate[:].rearrange("p g e t -> p (g e t)")[:, bass.ds((g * E + e) * GT + t, 1)]
                    m = nc.vector.scalar_tensor_tensor(out=z2[:, t, :], in0=bank[4 + par][:, t * P:(t + 1) * P], scalar=gcol,
                                                       in1=base, op0=ALU.mult, op1=ALU.add)
                m.then_inc(f_ac, 1)

            def out_norm(g):
                dve.wait_ge(f_ac, (g + 1) * E)
                for t in range(GT):
                    m = nc.vector.bn_stats(st[:, t, :], z2[:, t, :])
                m.then_inc(f_st, 1)
                wait_apart(dve, f_st, g + 1, prep, PREP)
                for t in range(GT):
                    m = nc.vector.bn_aggr(mv[:, t, :], st[:, t, :])
                m.then_inc(f_mv, 1)

            def out_fin(g):
                wait(dve, stored, g * 16)
                dve.wait_ge(f_rs, g + 1)
                for t in range(GT):
                    m = nc.vector.tensor_scalar(z[:, t, :], z2[:, t, :], mv[:, t, 0:1], rstd[:, t:t + 1], ALU.subtract, ALU.mult)
                m.then_inc(f_fin, 1)

            def expert(g, e, par, first, head):
                low(g, e, 0)
                low(g, e, 1)
                if head and not first:
                    add(g - 1, E - 1, 1 - par, False)
                    out_norm(g - 1)
                elif not head:
                    add(g, e - 1, 1 - par, isinstance(e, int) and e == 1)
                low(g, e, 2)
                if head and not first:
                    out_fin(g - 1)
                low(g, e, 3)
            expert_loop(dve, expert)
            add(G - 1, E - 1, 1, False)
            out_norm(G - 1)
            out_fin(G - 1)


POOL_READY = 8 + 4 * 4 + 2
PREP = 9
SLOTS = {"self": {"XT": 0, "QK": 1, "V": 2, "AT": 2, "O": 3},
         "cross": {"XT": 0, "CT": 1, "QK": 2, "V": 3, "AT": 4, "O": 6}}


def slot(la, what):
    return SLOTS[la.name][what]


def kernel(x, ctx_1024, mask_BxSxS2_bf0, L0_attn_Wq, L0_attn_bq, L0_attn_Wk, L0_attn_bk, L0_attn_Wv, L0_attn_bv, L0_attn_Wo,
           L0_attn_bo, L0_xattn_Wq, L0_xattn_Wk, L0_xattn_Wv, L0_xattn_Wo, L0_ffn_W1, L0_ffn_W2, L0_ffn_Wr):
    import concourse.bacc as bacc
    from concourse.bass_utils import run_bass_kernel_spmd

    def by_head_pair(w, la):
        w = np.asarray(w).reshape(la.quads, 2, 2, la.dk, D)
        return w.transpose(2, 0, 1, 3, 4).reshape(D, D)

    wstack = np.stack([np.asarray(w) for w in (
        L0_attn_Wq, L0_attn_Wk, L0_attn_Wv, by_head_pair(L0_attn_Wo, SELF),
        np.asarray(L0_xattn_Wq).T, np.asarray(L0_xattn_Wk).T, np.asarray(L0_xattn_Wv).T, by_head_pair(np.asarray(L0_xattn_Wo).T, CROSS))])
    biases = np.concatenate([np.asarray(b) for b in (L0_attn_bq, L0_attn_bk, L0_attn_bv, L0_attn_bo)]).reshape(1, 4 * D)
    const = np.zeros((P, P + 16), np.float32)
    const[:, 0:P] = np.eye(P)
    for n, la in enumerate((SELF, CROSS)):
        for hc in range(4):
            const[:, P + 4 * n + hc] = (np.arange(P) % la.rows) // la.dk == hc
    const[:, P + 8:P + 16] = np.arange(E) - E
    arrays = {
        "x": np.asarray(x), "ctx_in": np.asarray(ctx_1024), "mask": np.asarray(mask_BxSxS2_bf0),
        "wstack": wstack, "biases": biases,
        "w1": np.asarray(L0_ffn_W1).reshape(E * DFF, D).T,
        "w2": np.asarray(L0_ffn_W2).reshape(E, D, FC, P).transpose(3, 0, 2, 1).reshape(P, E * FC * D),
        "wr": np.asarray(L0_ffn_Wr).T, "const": const,
    }
    nc = bacc.Bacc("TRN2", target_bir_lowering=False, num_devices=1)
    feeds, args = {}, []
    for name, a in arrays.items():
        feeds[f"{name}_dram"] = np.ascontiguousarray(a)
        args.append(nc.dram_tensor(f"{name}_dram", a.shape, mybir.dt.from_np(a.dtype), kind="ExternalInput").ap())
    args.append(nc.dram_tensor("out_dram", (B, S, D), F32, kind="ExternalOutput").ap())
    program(nc, *args)
    return run_bass_kernel_spmd(nc, [feeds], core_ids=[0]).results[0]["out_dram"]
```

```python
import numpy as np
import concourse.bass as bass
from concourse import mybir
from contextlib import ExitStack

F32, F16, BF16, U8, U32 = (mybir.dt.float32, mybir.dt.float16, mybir.dt.bfloat16, mybir.dt.uint8, mybir.dt.uint32)
ACT = mybir.ActivationFunctionType
ALU = mybir.AluOpType
AX = mybir.AxisListType

B, S, D = 128, 64, 128
TOK = B * S
P = 128
NT = TOK // P
GT = 4
GTOK = GT * P
G = NT // GT
GB = GTOK // S
HB = GB // 2
E, DFF, FC = 8, 512, 4
EPS = 1e-5
WS = 64.0
IWS = 1.0 / WS
BIG = float(2.0 ** 100)


class Layer:
    def __init__(self, name, heads, cross, w):
        self.name, self.cross = name, cross
        self.dk = D // heads
        self.quads = heads // 4
        self.nh = self.quads * 2
        self.wq, self.wk, self.wv, self.wo = w
        self.qclasses = 4 if cross else 2
        self.class_slots = {1: (0, 1, 2, 3), 3: (4, 5), 4: (6, 7)} if cross else {0: (0, 1), 1: (4, 5, 6, 7)}
        self.masks = 8 if cross else 0
        self.qscale = IWS * float(np.float32(self.dk ** -0.5))

    def classes(self, quad):
        return 2 * (quad // 2), 2 * (quad % 2)


SELF = Layer("self", 8, False, (0, 1, 2, 3))
CROSS = Layer("cross", 16, True, (4, 5, 6, 7))


def wait(eng, sem, value):
    if isinstance(value, int) and value <= 0:
        return
    eng.wait_ge(sem, value)


def wait_apart(eng, sem, value, reached, count):
    value = value if isinstance(value, int) else eng.to_reg(value)
    eng.wait_ge(reached, count)
    wait(eng, sem, value)


def first_group(g):
    return isinstance(g, int) and g == 0


def units(layer):
    return [(u // 2, u % 2) for u in range(layer.nh)]


def program(nc, x, ctx_in, mask, wstack, biases, w1, w2, wr, const, out):
    ctx = ExitStack()
    with ctx:
        def sb(name, shape, dt):
            return ctx.enter_context(nc.sbuf_tensor(name, shape, dt))

        def sem(name):
            return ctx.enter_context(nc.semaphore(name))

        X = sb("X", [P, NT, D], F32)
        ident = sb("ident", [P, P], F32)
        cst = sb("cst", [P, 24], F32)
        Wf = sb("Wf", [P, 8, D], F32)
        Wh = sb("Wh", [P, 8, D], F16)
        Wl = sb("Wl", [P, 8, D], F16)
        Wrf = sb("Wrf", [P, E], F32)
        Wrh = sb("Wrh", [P, E], F16)
        Wrl = sb("Wrl", [P, E], F16)
        bf = sb("bf", [2, 4 * D], F32)
        bh = sb("bh", [2, 4 * D], F16)
        bl = sb("bl", [2, 4 * D], F32)
        b2 = sb("b2", [P, 4 * D], F16)
        ones2 = sb("ones2", [P, GTOK], F16)
        bigI = sb("bigI", [P, P], BF16)
        negI = sb("negI", [P, P], BF16)
        W1h = sb("W1h", [P, E * DFF], F16)
        W1l = sb("W1l", [P, E * DFF], F16)
        W2h = sb("W2h", [P, E * DFF], F16)
        W2l = sb("W2l", [P, E * DFF], F16)
        wst = sb("wst", [P, E * DFF], F32)
        xth = [sb(f"xth{i}", [P, GTOK], F16) for i in range(2)]
        xtl = [sb(f"xtl{i}", [P, GTOK], F16) for i in range(2)]
        cin = [sb(f"cin{i}", [P, GT, D], F32) for i in range(2)]
        cth = [sb(f"cth{i}", [P, GTOK], F16) for i in range(2)]
        ctl = [sb(f"ctl{i}", [P, GTOK], F16) for i in range(2)]
        mraw = [sb(f"mraw{i}", [P, GB, S], U8) for i in range(2)]
        mbf = [sb(f"mbf{i}", [P, GB, S], BF16) for i in range(2)]
        qh = sb("qh", [P, GTOK], F16)
        ql = sb("ql", [P, GTOK], F16)
        qzh = [sb(f"qzh{i}", [P, GB, 4, S], F16) for i in range(2)]
        qzl = [sb(f"qzl{i}", [P, GB, 4, S], F16) for i in range(2)]
        kh = sb("kh", [P, GTOK], F16)
        kl = sb("kl", [P, GTOK], F16)
        vz = {}
        for la in (SELF, CROSS):
            for part in "hl":
                vz[la.name, part] = [sb(f"vz_{la.name}_{part}{i}", [P, 2, GT * la.quads, 2, 2, la.dk + 1], F16)
                                     for i in range(2)]
        pr = [sb(f"pr{i}", [P, 512], F32) for i in range(2)]
        pth = [sb(f"pth{i}", [P, 512], F16) for i in range(2)]
        ptl = [sb(f"ptl{i}", [P, 512], F16) for i in range(2)]
        mx = [sb(f"mx{i}", [P, 8], BF16) for i in range(2)]
        rc = [sb(f"rc{i}", [P, HB, 4], F32) for i in range(2)]
        at = [sb(f"at{i}", [P, GT, D], F32) for i in range(2)]
        ath = sb("ath", [P, GTOK], F16)
        atl = sb("atl", [P, GTOK], F16)
        xs = [sb(f"xs{i}", [P, GT, D], F32) for i in range(2)]
        z = sb("z", [P, GT, D], F32)
        z2 = sb("z2", [P, GT, D], F32)
        st = sb("st", [P, GT, 6], F32)
        mv = sb("mv", [P, GT, 2], F32)
        ve = sb("ve", [P, GT], F32)
        mhalf = sb("mhalf", [P, GT], F32)
        rstd = sb("rstd", [P, GT], F32)
        XTh = sb("XTh", [P, TOK], F16)
        XTl = sb("XTl", [P, TOK], F16)
        lg, prob, hot0, hot1 = (wst[:, n * NT * E:(n + 1) * NT * E].rearrange("p (t e) -> p t e", e=E) for n in range(4))
        hot = (hot0, hot1)
        rt = wst[:, 4 * NT * E:4 * NT * E + 7 * NT].rearrange("p (r t) -> p r t", t=NT)
        gate = sb("gate", [P, G, E, GT], F32)
        kzh, kzl = ([XTh[:, n * 4 * GTOK:(n + 1) * 4 * GTOK].rearrange("p (b c s) -> p b c s", b=GB, c=4) for n in (m, m + 1)]
                    for m in (0, 2))
        s32 = pr + [xs[i][:].rearrange("p t d -> p (t d)") for i in range(2)]
        sh = pth + xth
        sl = ptl + xtl

        bank = [ctx.enter_context(nc.psum_tensor(f"bank{i}", [P, 512], F32)) for i in range(8)]
        SC, TB, PVB, M0, M1 = bank[0:2], bank[2:4], bank[4:6], bank[6], bank[7]

        ld_x = [sem("ld_x0"), sem("ld_x1")]
        ld_w, ld_w1, ld_w2 = sem("ld_w"), sem("ld_w1"), sem("ld_w2")
        pool_ready, prep, wh_done, w1_split, w2_split = (sem(n) for n in "pool_ready prep wh_done w1_split w2_split".split())
        var_eps = sem("var_eps")
        ld_c = [sem("ld_c0"), sem("ld_c1")]
        ld_m = [sem("ld_m0"), sem("ld_m1")]
        mask_done = sem("mask_done")
        NAMES = ("xs xt xh xl ct ch cl q qh ql k kh klo kl kz v vh vl s mx inj ex t ph pl pv rc nm at ah al o zz st mv rs fin").split()
        sems = {la.name: {n: sem(f"{la.name}_{n}") for n in NAMES} for la in (SELF, CROSS)}
        r_xt, r_xh, r_xl, r_lg, r_lc = sem("r_xt"), sem("r_xh"), sem("r_xl"), sem("r_lg"), sem("r_lc")
        r_xs, r_sub, r_ex = sem("r_xs"), sem("r_sub"), sem("r_ex")
        f_h, f_si, f_sl, f_y, f_ac, f_st, f_mv, f_rs, f_fin, stored = (sem(n) for n in (
            "f_h f_si f_sl f_y f_ac f_st f_mv f_rs f_fin stored").split())

        block = ctx.enter_context(nc.Block())
        x_v = x.rearrange("b s d -> (b s) d").rearrange("(g t p) d -> g p t d", t=GT, p=P)
        c_v = ctx_in.rearrange("b s d -> (b s) d").rearrange("(g t p) d -> g p t d", t=GT, p=P)
        o_v = out.rearrange("b s d -> (b s) d").rearrange("(g t p) d -> g p t d", t=GT, p=P)
        m_v = mask.rearrange("(g b) q k -> g q b k", b=GB)

        def over_groups(eng, body):
            body(0, 0, G - 1)
            body(1, 1, G - 2)
            with eng.Fori(1, G // 2 - 1) as j:
                body(2 * j, 0, 2)
                body(2 * j + 1, 1, 2)
            for g in range(G - 2, G):
                body(g, g % 2, G - 1 - g)

        def expert_loop(eng, expert):
            def rest(g):
                with eng.Fori(1, E // 2) as j:
                    expert(g, 2 * j, 0, False, False)
                    expert(g, 2 * j + 1, 1, False, False)
            for g in range(2):
                expert(g, 0, 0, g == 0, True)
                expert(g, 1, 1, False, False)
                rest(g)
            with eng.Fori(2, G) as g:
                expert(g, 0, 0, False, True)
                expert(g, 1, 1, False, False)
                rest(g)

        def vsrc(la, b2_, jp):
            return M0[S * b2_:S * b2_ + S, :].rearrange("p (n j c d) -> p n j c d", j=2, c=2, d=la.dk)[:, :, jp]

        def vdst(la, part, i, b2_, jp):
            return vz[la.name, part][i][S * jp:S * jp + S, b2_, :, jp, :, 0:la.dk]

        @block.sync
        def _(sp):
            sp.dma_start(ident[:], const[:, 0:P]).then_inc(ld_w, 16)
            sp.dma_start(cst[:], const[:, P:P + 24]).then_inc(ld_w, 16)
            sp.dma_start(Wf[:], wstack.rearrange("w p d -> p w d")).then_inc(ld_w, 16)
            sp.dma_start(Wrf[:], wr).then_inc(ld_w, 16)
            sp.dma_start(bf[0:1, :], biases).then_inc(ld_w, 16)
            sp.dma_start(bf[1:2, :], biases).then_inc(ld_w, 16)
            for g in range(2):
                sp.dma_start(X[:, g * GT:(g + 1) * GT, :], x_v[g]).then_inc(ld_x[g], 16)
            with sp.Fori(1, G // 2) as j:
                for i in range(2):
                    wait_apart(sp, ld_x[i], 16 * j, ld_x[i], 16)
                    sp.dma_start(X[:, bass.ds((2 * j + i) * GT, GT), :], x_v[bass.ds(2 * j + i, 1)].rearrange("o p t d -> p (o t) d")).then_inc(ld_x[i], 16)
            sp.dma_start(wst[:], w1).then_inc(ld_w1, 16)
            for g in range(2):
                sp.dma_start(cin[g][:], c_v[g]).then_inc(ld_c[g], 16)
                for c in range(2):
                    sp.dma_start(mraw[g][S * c:S * c + S], m_v[g]).then_inc(ld_m[g], 16)
            sp.wait_ge(w1_split, 2)
            sp.dma_start(wst[:], w2).then_inc(ld_w2, 16)
            sc = sems["cross"]
            with sp.Fori(1, G // 2) as j:
                for i in range(2):
                    wait_apart(sp, sc["ct"], 2 * j + i - 1, ld_x[i], 16)
                    sp.dma_start(cin[i][:], c_v[bass.ds(2 * j + i, 1)].rearrange("o p t d -> p (o t) d")).then_inc(ld_c[i], 16)
                    wait_apart(sp, mask_done, 2 * j + i - 1, ld_x[i], 16)
                    for c in range(2):
                        sp.dma_start(mraw[i][S * c:S * c + S], m_v[bass.ds(2 * j + i, 1)].rearrange("o q b k -> q (o b) k")).then_inc(ld_m[i], 16)
            with sp.Fori(0, G) as g:
                wait_apart(sp, f_fin, g + 1, ld_x[0], 16)
                sp.dma_start(o_v[bass.ds(g, 1)].rearrange("o p t d -> p (o t) d"), z[:]).then_inc(stored, 16)
            sp.wait_ge(stored, 16 * G)

        @block.gpsimd
        def _(pool):
            nc.gpsimd.memset(ones2[:], 1.0).then_inc(pool_ready, 1)
            nc.gpsimd.memset(mhalf[:], -0.5).then_inc(pool_ready, 1)
            nc.gpsimd.memset(b2[:], 0.0).then_inc(pool_ready, 1)
            zeroed = [nc.gpsimd.memset(v[:].rearrange("p a b c d e -> p (a b c d e)"), 0.0).then_inc(pool_ready, 1)
                      for pair in vz.values() for v in pair]
            pool.wait_ge(pool_ready, 3 + len(zeroed))
            for la in (SELF, CROSS):
                for v in vz[la.name, "h"]:
                    for jp in range(2):
                        for par in range(2):
                            nc.gpsimd.memset(v[S * jp:S * jp + S, par, :, jp, :, la.dk:la.dk + 1], WS).then_inc(pool_ready, 1)

            def stage(g, i, done, transposed):
                if not isinstance(g, int) or g >= 2:
                    wait_apart(pool, transposed, g - 1, pool_ready, POOL_READY)
                nc.gpsimd.tensor_copy(xs[i][:], X[:, bass.ds(g * GT, GT), :]).then_inc(done, 1)

            def inv_std(g, stats_done, before, done):
                wait_apart(pool, stats_done, g + 1, pool_ready, POOL_READY)
                nc.gpsimd.tensor_scalar(ve[:], mv[:, :, 1], EPS, None, ALU.add).then_inc(var_eps, 1)
                pool.wait_ge(var_eps, before + g + 1)
                nc.gpsimd.tensor_tensor(rstd[:], ve[:], mhalf[:], ALU.pow).then_inc(done, 1)

            def convert(g, i):
                wait_apart(pool, ld_m[i], 16 * (g - i) + 32, pool_ready, POOL_READY)
                if not isinstance(g, int) or g >= 2:
                    wait_apart(pool, sems["cross"]["s"], (g - 1) * CROSS.nh, pool_ready, POOL_READY)
                nc.gpsimd.tensor_copy(mbf[i][:], mraw[i][:]).then_inc(mask_done, 1)

            def attention(la, before):
                s = sems[la.name]

                def ahead(g, i):
                    if not la.cross:
                        wait_apart(pool, ld_x[i], 8 * (g - i) + 16, pool_ready, POOL_READY)
                    stage(g, i, s["xs"], s["xt"])
                    if la.cross:
                        convert(g, i)

                def body(g, i, follow):
                    if follow >= 2:
                        ahead(g + 2, i)
                    if not first_group(g):
                        inv_std(g - 1, s["mv"], before, s["rs"])
                ahead(0, 0)
                ahead(1, 1)
                over_groups(pool, body)
                inv_std(G - 1, s["mv"], before, s["rs"])

            pool.wait_ge(pool_ready, POOL_READY)
            attention(SELF, 0)
            pool.wait_ge(sems["self"]["fin"], G)
            attention(CROSS, G)
            pool.wait_ge(sems["cross"]["fin"], G)
            for g in range(2):
                nc.gpsimd.tensor_copy(xs[g][:], X[:, g * GT:(g + 1) * GT, :]).then_inc(r_xs, 1)
            with pool.Fori(1, G // 2) as j:
                for i in range(2):
                    wait_apart(pool, r_xt, 2 * j + i - 1, pool_ready, POOL_READY)
                    nc.gpsimd.tensor_copy(xs[i][:], X[:, bass.ds((2 * j + i) * GT, GT), :]).then_inc(r_xs, 1)

            with pool.Fori(0, G) as g:
                inv_std(g, f_mv, 2 * G, f_rs)

        @block.tensor
        def _(pe):
            def three(out_, l, r, start=True, stop=True, last_inc=None, **kw):
                (lh, ll), (rh, rl) = l, r
                nc.tensor.matmul(out_, lh, rh, start=start, stop=False, **kw)
                nc.tensor.matmul(out_, lh, rl, start=False, stop=False, **kw)
                return nc.tensor.matmul(out_, ll, rh, start=False, stop=stop, **kw)

            def attention(la):
                s = sems[la.name]
                us = units(la)
                W = 4 * (la.dk + 1)

                def XT(g, i):
                    pe.wait_ge(s["xs"], g + 1)
                    wait(pe, s["vl"], g)
                    for t in range(GT):
                        m = nc.tensor.transpose(M0[:, t * P:(t + 1) * P], xs[i][:, t, :], ident[:])
                    m.then_inc(s["xt"], 1)

                def CT(g, i):
                    pe.wait_ge(ld_c[i], 8 * (g - i) + 16)
                    wait(pe, s["klo"], g)
                    wait(pe, s["zz"], g - 2)
                    for t in range(GT):
                        m = nc.tensor.transpose(M1[:, t * P:(t + 1) * P], cin[i][:, t, :], ident[:])
                    m.then_inc(s["ct"], 1)

                def proj(out_, w, r, bias, done):
                    m = three(out_, (Wh[:, w, :], Wl[:, w, :]), r, stop=bias is None)
                    if bias is not None:
                        m = nc.tensor.matmul(out_, b2[:, bias * D:(bias + 1) * D], ones2[:], start=False, stop=True)
                    m.then_inc(done, 1)

                def Qp(g, i):
                    pe.wait_ge(s["xl"], g + 1)
                    proj(M0[:], la.wq, (xth[i][:], xtl[i][:]), None if la.cross else 0, s["q"])

                def Kp(g, i):
                    if la.cross:
                        pe.wait_ge(s["cl"], g + 1)
                        proj(M1[:], la.wk, (cth[i][:], ctl[i][:]), None, s["k"])
                    else:
                        wait(pe, s["zz"], g - 2)
                        proj(M1[:], la.wk, (xth[i][:], xtl[i][:]), 1, s["k"])

                def Vp(g, i):
                    pe.wait_ge(s["ql"], g + 1)
                    src = (cth[i], ctl[i]) if la.cross else (xth[i], xtl[i])
                    for t in range(GT):
                        c = slice(t * P, (t + 1) * P)
                        m = three(M0[:, c], (src[0][:, c], src[1][:, c]), (Wh[:, la.wv, :], Wl[:, la.wv, :]), stop=la.cross)
                        if not la.cross:
                            m = nc.tensor.matmul(M0[:, c], ones2[:, 0:P], b2[:, 2 * D:3 * D], start=False, stop=True)
                    m.then_inc(s["v"], 1)

                def scores(g, u, i):
                    n = g * la.nh + u
                    quad, half = us[u]
                    qc, kc = la.classes(quad)
                    wait(pe, s["ex"], n - 1)
                    if u == 0:
                        pe.wait_ge(s["kl"], g + 1)
                        pe.wait_ge(s["kz"], g + 1)
                    bnk = SC[u % 2]
                    if la.cross:
                        if u == 0:
                            pe.wait_ge(mask_done, g + 1)
                        nc.tensor.matmul(bnk[:].rearrange("p (b j k) -> p b j k", b=HB, j=2), bigI[:],
                                         mbf[i][:, half * HB:(half + 1) * HB, :].unsqueeze(2).to_broadcast([P, HB, 2, S]),
                                         start=True, stop=False, skip_group_check=True)
                    for b in range(HB):
                        bb = half * HB + b
                        l = [q[i][:, bb, qc:qc + 2, :].rearrange("p c s -> p (c s)") for q in (qzh, qzl)]
                        r = [k[i][:, bb, kc:kc + 2, :].rearrange("p c s -> p (c s)") for k in (kzh, kzl)]
                        m = three(bnk[:, b * P:(b + 1) * P], l, r, start=b == 0 and not la.cross, stop=False, skip_group_check=True)
                    m.then_inc(s["s"], 1)

                def less_max(g, u):
                    pe.wait_ge(s["mx"], g * la.nh + u + 1)
                    nc.tensor.matmul(SC[u % 2][:].rearrange("p (r k) -> p r k", k=S), negI[:],
                                     mx[u % 2][:].unsqueeze(2).to_broadcast([P, 8, S]),
                                     start=False, stop=True, skip_group_check=True).then_inc(s["inj"], 1)

                def flip(g, u, i):
                    n = g * la.nh + u
                    pe.wait_ge(s["ex"], n + 1)
                    wait(pe, s["pl"], n - 1)
                    for b in range(HB):
                        m = nc.tensor.transpose(TB[u % 2][:, b * P:(b + 1) * P], pr[u % 2][:, b * P:(b + 1) * P], ident[:])
                    m.then_inc(s["t"], 1)

                def values(g, u, i):
                    n = g * la.nh + u
                    quad, half = us[u]
                    pe.wait_ge(s["pl"], n + 1)
                    wait(pe, s["nm"], n - 1)
                    if u == 0:
                        pe.wait_ge(s["vl"], g + 1)
                    for b in range(HB):
                        bb = half * HB + b
                        c = slice(b * P, (b + 1) * P)
                        v = [vz[la.name, part][i][:, bb % 2, (bb // 2) * la.quads + quad].rearrange("p j c d -> p (j c d)") for part in "hl"]
                        m = three(PVB[u % 2][:, b * W:(b + 1) * W], (pth[u % 2][:, c], ptl[u % 2][:, c]), v)
                    m.then_inc(s["pv"], 1)

                def AT(g, i):
                    pe.wait_ge(s["nm"], (g + 1) * la.nh)
                    pe.wait_ge(s["klo"], min(g + 3, G) if isinstance(g, int) else g + 3)
                    for t in range(GT):
                        m = nc.tensor.transpose(M1[:, t * P:(t + 1) * P], at[i][:, t, :], ident[:])
                    m.then_inc(s["at"], 1)

                def O(g, i):
                    pe.wait_ge(s["al"], g + 1)
                    for t in range(GT):
                        c = slice(t * P, (t + 1) * P)
                        m = three(M1[:, c], (ath[:, c], atl[:, c]), (Wh[:, la.wo, :], Wl[:, la.wo, :]), stop=la.cross)
                        if not la.cross:
                            m = nc.tensor.matmul(M1[:, c], ones2[:, 0:P], b2[:, 3 * D:4 * D], start=False, stop=True)
                    m.then_inc(s["o"], 1)

                def body(g, i, follow):
                    first = first_group(g)
                    for u in range(la.nh):
                        flip(g, u, i)
                        if u > 0:
                            values(g, u - 1, i)
                        elif not first:
                            values(g - 1, la.nh - 1, 1 - i)
                        if u + 1 < la.nh:
                            less_max(g, u + 1)
                        elif follow:
                            less_max(g + 1, 0)
                        if u + 2 < la.nh:
                            scores(g, u + 2, i)
                        elif follow:
                            scores(g + 1, u + 2 - la.nh, 1 - i)
                        if follow:
                            if u == slot(la, "QK"):
                                Qp(g + 1, 1 - i)
                                Kp(g + 1, 1 - i)
                            if u == slot(la, "V"):
                                Vp(g + 1, 1 - i)
                        if u == slot(la, "AT") and not first:
                            AT(g - 1, 1 - i)
                        if u == slot(la, "O") and not first:
                            O(g - 1, 1 - i)
                        if follow >= 2:
                            if u == slot(la, "XT"):
                                XT(g + 2, i)
                            if la.cross and u == slot(la, "CT"):
                                CT(g + 2, i)

                XT(0, 0)
                if la.cross:
                    CT(0, 0)
                Qp(0, 0)
                Kp(0, 0)
                Vp(0, 0)
                XT(1, 1)
                if la.cross:
                    CT(1, 1)
                scores(0, 0, 0)
                scores(0, 1, 0)
                less_max(0, 0)
                over_groups(pe, body)
                values(G - 1, la.nh - 1, 1)
                AT(G - 1, 1)
                O(G - 1, 1)

            pe.wait_ge(prep, PREP)
            attention(SELF)
            pe.wait_ge(sems["self"]["fin"], G)
            attention(CROSS)

            pe.wait_ge(sems["cross"]["fin"], G)
            pe.wait_ge(prep, PREP)

            def rows_ahead(g, i):
                pe.wait_ge(r_xs, g + 1)
                for t in range(GT):
                    m = nc.tensor.transpose(bank[i][:, t * P:(t + 1) * P], xs[i][:, t, :], ident[:])
                m.then_inc(r_xt, 1)

            def logits(g, i):
                pe.wait_ge(r_xl, g + 1)
                if not isinstance(g, int) or g >= 2:
                    pe.wait_ge(r_lc, g - 1)
                for t in range(GT):
                    rows = [q[:, bass.ds(g * GTOK + t * P, P)] for q in (XTh, XTl)]
                    m = three(bank[2 + i][:, t * E:(t + 1) * E], rows, (Wrh[:], Wrl[:]))
                m.then_inc(r_lg, 1)

            rows_ahead(0, 0)
            rows_ahead(1, 1)
            logits(0, 0)

            def pair(j):
                rows_ahead(2 * j + 2, 0)
                logits(2 * j + 1, 1)
                rows_ahead(2 * j + 3, 1)
                logits(2 * j + 2, 0)
            pair(0)
            with pe.Fori(1, (G - 2) // 2) as j:
                pair(j)
            logits(G - 1, 1)
            pe.wait_ge(r_lc, G)

            H, Y = bank[0:4], bank[4:6]

            def up(g, e, f):
                n = g * (E * FC) + e * FC + f
                wait(pe, f_si, n - 3)
                cols = bass.ds(e * DFF + f * P, P)
                rows = [q[:, bass.ds(g * GTOK, GTOK)] for q in (XTh, XTl)]
                three(H[f][:], (W1h[:, cols], W1l[:, cols]), rows).then_inc(f_h, 1)

            def down(g, e, f, par):
                n = g * (E * FC) + e * FC + f
                pe.wait_ge(f_sl, n + 1)
                if f == 0:
                    wait(pe, f_ac, g * E + e - 1)
                cols = bass.ds((e * FC + f) * D, D)
                for t in range(GT):
                    c = slice(t * P, (t + 1) * P)
                    m = three(Y[par][:, c], (sh[f][:, c], sl[f][:, c]), (W2h[:, cols], W2l[:, cols]),
                              start=(f == 0 and t == 0), stop=(f == FC - 1), skip_group_check=True)
                if f == FC - 1:
                    m.then_inc(f_y, 1)

            def expert(g, e, par, first, head):
                for f in range(FC):
                    up(g, e, f)
                    if f >= 2:
                        down(g, e, f - 2, par)
                    elif head and not first:
                        down(g - 1, E - 1, f + 2, 1 - par)
                    elif not first:
                        down(g, e - 1, f + 2, 1 - par)

            pe.wait_ge(w1_split, 2)
            pe.wait_ge(w2_split, 2)
            expert_loop(pe, expert)
            down(G - 1, E - 1, 2, 1)
            down(G - 1, E - 1, 3, 1)

        @block.scalar
        def _(act):
            act.wait_ge(ld_w, 96)
            nc.scalar.activation(Wh[:], Wf[:], ACT.Copy, scale=WS).then_inc(wh_done, 1)

            def attention(la):
                s = sems[la.name]
                us = units(la)

                def xh(g, i):
                    act.wait_ge(s["xt"], g + 1)
                    nc.scalar.activation(xth[i][:], M0[:], ACT.Copy).then_inc(s["xh"], 1)

                def ch(g, i):
                    act.wait_ge(s["ct"], g + 1)
                    nc.scalar.activation(cth[i][:], M1[:], ACT.Copy).then_inc(s["ch"], 1)

                def qkh(g, i):
                    act.wait_ge(s["q"], g + 1)
                    nc.scalar.activation(qh[:], M0[:], ACT.Copy, scale=la.qscale).then_inc(s["qh"], 1)
                    act.wait_ge(s["k"], g + 1)
                    nc.scalar.activation(kh[:], M1[:], ACT.Copy, scale=IWS).then_inc(s["kh"], 1)

                def classes(g, i, part):
                    act.wait_ge(s["qh"], g + 1)
                    act.wait_ge(s["kh"], g + 1)
                    for c in part:
                        src, dst, c = (qh, qzh[i], c) if c < 4 else (kh, kzh[i], c - 4)
                        k = la.masks + c + (0 if src is qh else 4)
                        m = nc.scalar.activation(dst[:, :, c, :], src[:].rearrange("p (b s) -> p b s", b=GB), ACT.Copy,
                                                 scale=cst[:, k:k + 1])
                    if part[-1] == 7:
                        m.then_inc(s["kz"], 1)

                def vh(g, i):
                    act.wait_ge(s["v"], g + 1)
                    for b2_ in range(2):
                        for jp in range(2):
                            m = nc.scalar.activation(vdst(la, "h", i, b2_, jp), vsrc(la, b2_, jp), ACT.Copy)
                    m.then_inc(s["vh"], 1)

                def ex(g, u):
                    act.wait_ge(s["inj"], g * la.nh + u + 1)
                    nc.scalar.activation(pr[u % 2][:], SC[u % 2][:], ACT.Exp).then_inc(s["ex"], 1)

                def ph(g, u):
                    act.wait_ge(s["t"], g * la.nh + u + 1)
                    nc.scalar.activation(pth[u % 2][:], TB[u % 2][:], ACT.Copy).then_inc(s["ph"], 1)

                def ah(g):
                    act.wait_ge(s["at"], g + 1)
                    nc.scalar.activation(ath[:], M1[:], ACT.Copy).then_inc(s["ah"], 1)

                def body(g, i, follow):
                    for u in range(la.nh):
                        ph(g, u)
                        if u + 1 < la.nh:
                            ex(g, u + 1)
                        elif follow:
                            ex(g + 1, 0)
                        if follow:
                            if u == slot(la, "QK"):
                                qkh(g + 1, 1 - i)
                            if u == slot(la, "V"):
                                vh(g + 1, 1 - i)
                        if u == slot(la, "AT") and not first_group(g):
                            ah(g - 1)
                        if follow >= 2:
                            if u == slot(la, "XT"):
                                xh(g + 2, i)
                            if la.cross and u == slot(la, "CT"):
                                ch(g + 2, i)
                        if follow and u in la.class_slots:
                            classes(g + 1, 1 - i, la.class_slots[u])

                xh(0, 0)
                if la.cross:
                    ch(0, 0)
                qkh(0, 0)
                for part in la.class_slots.values():
                    classes(0, 0, part)
                vh(0, 0)
                xh(1, 1)
                if la.cross:
                    ch(1, 1)
                ex(0, 0)
                over_groups(act, body)
                ah(G - 1)

            act.wait_ge(pool_ready, POOL_READY)
            attention(SELF)
            attention(CROSS)

            def route(g, i):
                act.wait_ge(r_xt, g + 1)
                nc.scalar.activation(XTh[:, bass.ds(g * GTOK, GTOK)], bank[i][:], ACT.Copy).then_inc(r_xh, 1)
            with act.Fori(0, G // 2) as j:
                route(2 * j, 0)
                route(2 * j + 1, 1)
            act.wait_ge(r_sub, 1)
            nc.scalar.activation(prob, lg, ACT.Exp).then_inc(r_ex, 1)

            def silu(g, e, f):
                n = g * (E * FC) + e * FC + f
                act.wait_ge(f_h, n + 1)
                wait(act, f_sl, n - 3)
                nc.scalar.activation(s32[f][:], bank[f][:], ACT.Silu, scale=IWS)
                nc.scalar.activation(sh[f][:], bank[f][:], ACT.Silu, scale=IWS).then_inc(f_si, 1)

            def expert(g, e, par, first, head):
                for f in range(FC):
                    silu(g, e, f)
            expert_loop(act, expert)

        @block.vector
        def _(dve):
            links = [0]

            def link(ins):
                links[0] += 1
                ins.then_inc(prep, 1)
                dve.wait_ge(prep, links[0])

            dve.wait_ge(ld_w, 96)
            dve.wait_ge(pool_ready, POOL_READY)
            dve.wait_ge(wh_done, 1)
            link(nc.vector.scalar_tensor_tensor(out=Wl[:], in0=Wf[:], scalar=WS, in1=Wh[:], op0=ALU.mult, op1=ALU.subtract))
            link(nc.vector.tensor_scalar(Wrh[:], Wrf[:], WS, None, ALU.mult))
            link(nc.vector.scalar_tensor_tensor(out=Wrl[:], in0=Wrf[:], scalar=WS, in1=Wrh[:], op0=ALU.mult, op1=ALU.subtract))
            link(nc.vector.tensor_scalar(bigI[:], ident[:], -BIG, None, ALU.mult))
            link(nc.vector.tensor_scalar(negI[:], ident[:], -1.0, None, ALU.mult))
            link(nc.vector.tensor_scalar(bh[:], bf[:], WS, None, ALU.mult))
            link(nc.vector.scalar_tensor_tensor(out=bl[:], in0=bf[:], scalar=WS, in1=bh[:], op0=ALU.mult, op1=ALU.subtract))
            link(nc.vector.tensor_scalar(bf[:], bl[:], ident[0:2, 1:2], None, ALU.mult))
            link(nc.vector.scalar_tensor_tensor(out=b2[0:2, :], in0=bh[:], scalar=ident[0:2, 0:1], in1=bf[:], op0=ALU.mult, op1=ALU.add))
            assert links[0] == PREP

            def split_w(dst_h, dst_l, ready, done):
                dve.wait_ge(ready, 16)
                nc.vector.tensor_scalar(dst_h[:], wst[:], WS, None, ALU.mult).then_inc(done, 1)
                dve.wait_ge(done, 1)
                nc.vector.scalar_tensor_tensor(out=dst_l[:], in0=wst[:], scalar=WS, in1=dst_h[:], op0=ALU.mult, op1=ALU.subtract).then_inc(done, 1)

            def attention(la):
                s = sems[la.name]
                us = units(la)
                W = 4 * (la.dk + 1)

                def low(dst, psum, high, scale, done):
                    nc.vector.scalar_tensor_tensor(out=dst, in0=psum, scalar=scale, in1=high, op0=ALU.mult, op1=ALU.subtract).then_inc(done, 1)

                def xl(g, i):
                    dve.wait_ge(s["xh"], g + 1)
                    nc.vector.tensor_tensor(xtl[i][:], M0[:], xth[i][:], ALU.subtract).then_inc(s["xl"], 1)

                def cl(g, i):
                    dve.wait_ge(s["ch"], g + 1)
                    nc.vector.tensor_tensor(ctl[i][:], M1[:], cth[i][:], ALU.subtract).then_inc(s["cl"], 1)

                def qkl(g, i):
                    dve.wait_ge(s["qh"], g + 1)
                    low(ql[:], M0[:], qh[:], la.qscale, s["ql"])
                    dve.wait_ge(s["kh"], g + 1)
                    low(kl[:], M1[:], kh[:], IWS, s["klo"])

                def classes(g, i, part):
                    dve.wait_ge(s["ql"], g + 1)
                    dve.wait_ge(s["klo"], g + 1)
                    for c in part:
                        src, dst, c = (ql, qzl[i], c) if c < 4 else (kl, kzl[i], c - 4)
                        k = la.masks + c + (0 if src is ql else 4)
                        m = nc.vector.tensor_scalar(dst[:, :, c, :], src[:].rearrange("p (b s) -> p b s", b=GB),
                                                    cst[:, k:k + 1], None, ALU.mult)
                    if part[-1] == 7:
                        m.then_inc(s["kl"], 1)

                def vl(g, i):
                    dve.wait_ge(s["vh"], g + 1)
                    for b2_ in range(2):
                        for jp in range(2):
                            m = nc.vector.tensor_tensor(vdst(la, "l", i, b2_, jp), vsrc(la, b2_, jp), vdst(la, "h", i, b2_, jp), ALU.subtract)
                    m.then_inc(s["vl"], 1)

                def top(g, u):
                    n = g * la.nh + u
                    dve.wait_ge(s["s"], n + 1)
                    nc.vector.tensor_reduce(mx[u % 2][:], SC[u % 2][:].rearrange("p (r k) -> p r k", k=S), AX.X, ALU.max).then_inc(s["mx"], 1)

                def pl(g, u):
                    dve.wait_ge(s["ph"], g * la.nh + u + 1)
                    nc.vector.tensor_tensor(ptl[u % 2][:], TB[u % 2][:], pth[u % 2][:], ALU.subtract).then_inc(s["pl"], 1)

                def norm(g, u, i):
                    n = g * la.nh + u
                    quad, half = us[u]
                    dve.wait_ge(s["pv"], n + 1)
                    pv = PVB[u % 2][:, 0:HB * W].rearrange("p (b jc e) -> p b jc e", b=HB, jc=4)
                    nc.vector.reciprocal(rc[u % 2][:], pv[:, :, :, la.dk]).then_inc(s["rc"], 1)
                    dve.wait_ge(s["rc"], n + 1)
                    for c in range(2):
                        for b2_ in range(2):
                            rows = slice(S * c, S * c + S)
                            src = PVB[u % 2][rows, 0:HB * W].rearrange("p (t b j c e) -> p t b j c e", t=HB // 2, b=2, j=2, c=2)[:, :, b2_, :, c, 0:la.dk]
                            r = rc[u % 2][rows].rearrange("p (t b) (j c) -> p t b j c", b=2, c=2)[:, :, b2_, :, c].unsqueeze(3).to_broadcast([S, HB // 2, 2, la.dk])
                            dst = at[i][S * b2_:S * b2_ + S, half * 2:half * 2 + 2, :].rearrange(
                                "p t (c n j e) -> p t c n j e", c=2, n=la.quads, j=2)[:, :, c, quad]
                            m = nc.vector.tensor_tensor(dst, src, r, ALU.mult)
                    m.then_inc(s["nm"], 1)

                def al(g):
                    dve.wait_ge(s["ah"], g + 1)
                    nc.vector.tensor_tensor(atl[:], M1[:], ath[:], ALU.subtract).then_inc(s["al"], 1)

                def xg(g):
                    return X[:, bass.ds(g * GT, GT), :]

                def stats(g):
                    dve.wait_ge(s["o"], g + 1)
                    nc.vector.scalar_tensor_tensor(out=z[:], in0=M1[:].rearrange("p (t d) -> p t d", t=GT), scalar=IWS, in1=xg(g),
                                                   op0=ALU.mult, op1=ALU.add).then_inc(s["zz"], 1)
                    dve.wait_ge(s["zz"], g + 1)
                    layer_stats(s["st"], s["mv"], g)

                def finish(g):
                    layer_norm(s["rs"], g, xg(g), s["fin"])

                def body(g, i, follow):
                    first = first_group(g)
                    for u in range(la.nh):
                        if u == slot(la, "O") + 1 and not first:
                            stats(g - 1)
                        if u > 0:
                            norm(g, u - 1, i)
                        elif not first:
                            norm(g - 1, la.nh - 1, 1 - i)
                        pl(g, u)
                        if u + 2 < la.nh:
                            top(g, u + 2)
                        elif follow:
                            top(g + 1, u + 2 - la.nh)
                        if follow:
                            if u == slot(la, "QK"):
                                qkl(g + 1, 1 - i)
                            if u == slot(la, "V"):
                                vl(g + 1, 1 - i)
                        if u == slot(la, "AT") and not first:
                            al(g - 1)
                        if follow >= 2:
                            if u == slot(la, "XT"):
                                xl(g + 2, i)
                            if la.cross and u == slot(la, "CT"):
                                cl(g + 2, i)
                        if follow and u in la.class_slots:
                            classes(g + 1, 1 - i, la.class_slots[u])
                        if u == slot(la, "O") + 1 and not first:
                            finish(g - 1)

                xl(0, 0)
                if la.cross:
                    cl(0, 0)
                qkl(0, 0)
                for part in la.class_slots.values():
                    classes(0, 0, part)
                vl(0, 0)
                xl(1, 1)
                if la.cross:
                    cl(1, 1)
                top(0, 0)
                top(0, 1)
                over_groups(dve, body)
                norm(G - 1, la.nh - 1, 1)
                al(G - 1)
                stats(G - 1)
                finish(G - 1)

            def layer_stats(st_sem, mv_sem, g):
                for t in range(GT):
                    m = nc.vector.bn_stats(st[:, t, :], z[:, t, :])
                m.then_inc(st_sem, 1)
                wait_apart(dve, st_sem, g + 1, prep, PREP)
                for t in range(GT):
                    m = nc.vector.bn_aggr(mv[:, t, :], st[:, t, :])
                m.then_inc(mv_sem, 1)

            def layer_norm(rs_sem, g, dst, done):
                dve.wait_ge(rs_sem, g + 1)
                for t in range(GT):
                    m = nc.vector.tensor_scalar(dst[:, t, :], z[:, t, :], mv[:, t, 0:1], rstd[:, t:t + 1], ALU.subtract, ALU.mult)
                m.then_inc(done, 1)

            attention(SELF)
            split_w(W1h, W1l, ld_w1, w1_split)
            split_w(W2h, W2l, ld_w2, w2_split)
            attention(CROSS)

            def route(g, i):
                dve.wait_ge(r_xh, g + 1)
                cols = bass.ds(g * GTOK, GTOK)
                nc.vector.tensor_tensor(XTl[:, cols], bank[i][:], XTh[:, cols], ALU.subtract).then_inc(r_xl, 1)
                dve.wait_ge(r_lg, g + 1)
                nc.vector.tensor_scalar(lg[:, bass.ds(g * GT, GT), :], bank[2 + i][:, 0:GT * E].rearrange("p (t e) -> p t e", t=GT),
                                        IWS, None, ALU.mult).then_inc(r_lc, 1)
            with dve.Fori(0, G // 2) as j:
                route(2 * j, 0)
                route(2 * j + 1, 1)
            dve.wait_ge(r_lc, G)
            def each(v):
                return v.unsqueeze(2).to_broadcast([P, NT, E])

            link(nc.vector.tensor_reduce(rt[:, 0], lg, AX.X, ALU.max))
            nc.vector.tensor_tensor(lg, lg, each(rt[:, 0]), ALU.subtract).then_inc(r_sub, 1)
            dve.wait_ge(r_ex, 1)
            link(nc.vector.tensor_reduce(rt[:, 1], prob, AX.X, ALU.add))
            link(nc.vector.reciprocal(rt[:, 2], rt[:, 1]))
            link(nc.vector.tensor_tensor(prob, prob, each(rt[:, 2]), ALU.mult))
            rank = cst[:, 16:24].unsqueeze(1).to_broadcast([P, NT, E])
            for k in range(2):
                top, first = rt[:, 3 + k], rt[:, 5 + k]
                link(nc.vector.tensor_reduce(top, prob, AX.X, ALU.max))
                link(nc.vector.tensor_tensor(hot[k], prob, each(top), ALU.is_equal))
                link(nc.vector.tensor_tensor(hot[k], hot[k], rank, ALU.mult))
                link(nc.vector.tensor_reduce(first, hot[k], AX.X, ALU.min))
                link(nc.vector.tensor_tensor(hot[k], rank, each(first), ALU.is_equal))
                if k == 0:
                    link(nc.vector.scalar_tensor_tensor(out=prob, in0=hot[k], scalar=-2.0, in1=prob, op0=ALU.mult, op1=ALU.add))
            link(nc.vector.tensor_tensor(rt[:, 0], rt[:, 3], rt[:, 4], ALU.add))
            link(nc.vector.reciprocal(rt[:, 1], rt[:, 0]))
            for k in range(2):
                link(nc.vector.scalar_tensor_tensor(out=rt[:, 5 + k], in0=rt[:, 3 + k], scalar=IWS, in1=rt[:, 1], op0=ALU.mult, op1=ALU.mult))
                link(nc.vector.tensor_tensor(hot[k], hot[k], each(rt[:, 5 + k]), ALU.mult))
            link(nc.vector.tensor_tensor(gate[:].rearrange("p g e t -> p g t e"), hot[0].rearrange("p (g t) e -> p g t e", t=GT),
                                         hot[1].rearrange("p (g t) e -> p g t e", t=GT), ALU.add))

            def low(g, e, f):
                n = g * (E * FC) + e * FC + f
                dve.wait_ge(f_si, n + 1)
                nc.vector.tensor_tensor(sl[f][:], s32[f][:], sh[f][:], ALU.subtract).then_inc(f_sl, 1)

            def add(g, e, par, fresh):
                m_ = g * E + e
                dve.wait_ge(f_y, m_ + 1)
                if not fresh:
                    dve.wait_ge(f_ac, m_)
                for t in range(GT):
                    base = X[:, bass.ds(g * GT + t, 1), :].rearrange("p o d -> p (o d)") if fresh else z2[:, t, :]
                    gcol = gate[:].rearrange("p g e t -> p (g e t)")[:, bass.ds((g * E + e) * GT + t, 1)]
                    m = nc.vector.scalar_tensor_tensor(out=z2[:, t, :], in0=bank[4 + par][:, t * P:(t + 1) * P], scalar=gcol,
                                                       in1=base, op0=ALU.mult, op1=ALU.add)
                m.then_inc(f_ac, 1)

            def out_norm(g):
                dve.wait_ge(f_ac, (g + 1) * E)
                for t in range(GT):
                    m = nc.vector.bn_stats(st[:, t, :], z2[:, t, :])
                m.then_inc(f_st, 1)
                wait_apart(dve, f_st, g + 1, prep, PREP)
                for t in range(GT):
                    m = nc.vector.bn_aggr(mv[:, t, :], st[:, t, :])
                m.then_inc(f_mv, 1)

            def out_fin(g):
                wait(dve, stored, g * 16)
                dve.wait_ge(f_rs, g + 1)
                for t in range(GT):
                    m = nc.vector.tensor_scalar(z[:, t, :], z2[:, t, :], mv[:, t, 0:1], rstd[:, t:t + 1], ALU.subtract, ALU.mult)
                m.then_inc(f_fin, 1)

            def expert(g, e, par, first, head):
                low(g, e, 0)
                low(g, e, 1)
                if head and not first:
                    add(g - 1, E - 1, 1 - par, False)
                    out_norm(g - 1)
                elif not head:
                    add(g, e - 1, 1 - par, isinstance(e, int) and e == 1)
                low(g, e, 2)
                if head and not first:
                    out_fin(g - 1)
                low(g, e, 3)
            expert_loop(dve, expert)
            add(G - 1, E - 1, 1, False)
            out_norm(G - 1)
            out_fin(G - 1)


POOL_READY = 8 + 4 * 4 + 3
PREP = 9
SLOTS = {"self": {"QK": 0, "V": 1, "AT": 1, "O": 2, "XT": 3},
         "cross": {"QK": 0, "V": 2, "AT": 3, "O": 4, "XT": 5, "CT": 6}}


def slot(la, what):
    return SLOTS[la.name][what]


def kernel(x, ctx_1024, mask_BxSxS2_bf0, L0_attn_Wq, L0_attn_bq, L0_attn_Wk, L0_attn_bk, L0_attn_Wv, L0_attn_bv, L0_attn_Wo,
           L0_attn_bo, L0_xattn_Wq, L0_xattn_Wk, L0_xattn_Wv, L0_xattn_Wo, L0_ffn_W1, L0_ffn_W2, L0_ffn_Wr):
    import concourse.bacc as bacc
    from concourse.bass_utils import run_bass_kernel_spmd

    def by_head_pair(w, la):
        w = np.asarray(w).reshape(la.quads, 2, 2, la.dk, D)
        return w.transpose(2, 0, 1, 3, 4).reshape(D, D)

    wstack = np.stack([np.asarray(w) for w in (
        L0_attn_Wq, L0_attn_Wk, L0_attn_Wv, by_head_pair(L0_attn_Wo, SELF),
        np.asarray(L0_xattn_Wq).T, np.asarray(L0_xattn_Wk).T, np.asarray(L0_xattn_Wv).T, by_head_pair(np.asarray(L0_xattn_Wo).T, CROSS))])
    biases = np.concatenate([np.asarray(b) for b in (L0_attn_bq, L0_attn_bk, L0_attn_bv, L0_attn_bo)]).reshape(1, 4 * D)
    const = np.zeros((P, P + 24), np.float32)
    const[:, 0:P] = np.eye(P)
    for la in (SELF, CROSS):
        head = np.arange(P) // la.dk
        quad, pair, second = head // 4, head % 4 // 2, head % 2
        for c in range(4):
            const[:, P + la.masks + c] = 2 * (quad // 2) + second == c
            const[:, P + la.masks + 4 + c] = 2 * (quad % 2) + pair == c
    const[:, P + 16:P + 24] = np.arange(E) - E
    arrays = {
        "x": np.asarray(x), "ctx_in": np.asarray(ctx_1024), "mask": np.asarray(mask_BxSxS2_bf0),
        "wstack": wstack, "biases": biases,
        "w1": np.asarray(L0_ffn_W1).reshape(E * DFF, D).T,
        "w2": np.asarray(L0_ffn_W2).reshape(E, D, FC, P).transpose(3, 0, 2, 1).reshape(P, E * FC * D),
        "wr": np.asarray(L0_ffn_Wr).T, "const": const,
    }
    nc = bacc.Bacc("TRN2", target_bir_lowering=False, num_devices=1)
    feeds, args = {}, []
    for name, a in arrays.items():
        feeds[f"{name}_dram"] = np.ascontiguousarray(a)
        args.append(nc.dram_tensor(f"{name}_dram", a.shape, mybir.dt.from_np(a.dtype), kind="ExternalInput").ap())
    args.append(nc.dram_tensor("out_dram", (B, S, D), F32, kind="ExternalOutput").ap())
    program(nc, *args)
    return run_bass_kernel_spmd(nc, [feeds], core_ids=[0]).results[0]["out_dram"]
```
